# Optimizing a Trainium2 kernel written in Bass

```python
import numpy as np
import jax
import jax.numpy as jnp

def _softmax(x, axis=-1):
    return jax.nn.softmax(x, axis=axis)

def _gelu(x):
    return jax.nn.gelu(x, approximate=True)

def _silu(x):
    return jax.nn.silu(x)

def _sigmoid(x):
    return jax.nn.sigmoid(x)

def _layernorm(x, axis=-1, eps=1e-05):
    m = jnp.mean(x, axis=axis, keepdims=True)
    v = jnp.var(x, axis=axis, keepdims=True)
    return (x - m) / jnp.sqrt(v + eps)

def _scatter_add(tgt, idx, src, axis=0):
    return tgt.at[idx].add(src)

def _segment_sum(src, seg, n):
    return jax.ops.segment_sum(src, seg, n)
kernel_name = 'mk_audio_tower_d1_tok_audfeat512_r4_846b75'

def setup_inputs(seed: int=0):
    np.random.seed(seed)
    _w = jnp.asarray

    def _rec_inputs():
        import jax
        import jax.numpy as jnp
        _rk = jax.random.key(seed)
        x = -0.000392918 + 0.999932 * jax.random.normal(jax.random.fold_in(_rk, 1), (64, 125, 32), jnp.float32)
        return x
    x = _rec_inputs()

    def _L0_tok_setup():
        import jax, jax.numpy as jnp
        import numpy as np
        PATCH_LEN = 16
        STRIDE = 8
        IN_FEATS = 32
        D_MODEL = 128
        key = jax.random.key(seed)
        k1, k2, k3 = jax.random.split(key, 3)
        B, L, F = (128, 1024, IN_FEATS)
        x = jax.random.normal(k1, (B, L, F), dtype=jnp.float32)
        fan_in = IN_FEATS * PATCH_LEN
        bound = 1.0 / np.sqrt(fan_in)
        W = jax.random.uniform(k2, (D_MODEL, fan_in), dtype=jnp.float32, minval=-bound, maxval=bound)
        b = jax.random.uniform(k3, (D_MODEL,), dtype=jnp.float32, minval=-bound, maxval=bound)
        return {'x': x, 'W': W, 'b': b}
    _L0_tok_all = _L0_tok_setup()
    _L0_tok_in = {k: v for k, v in _L0_tok_all.items() if k in ('W', 'b')}
    del _L0_tok_all

    def _L0_attn_setup():
        import jax, jax.numpy as jnp
        import numpy as np
        NUM_HEAD = 8
        DIM_MODEL = 128
        DIM_HEAD = DIM_MODEL // NUM_HEAD
        LN_EPS = 1e-05
        key = jax.random.key(seed)
        ks = jax.random.split(key, 12)
        B, L, D = (4, 512, DIM_MODEL)
        s = 0.02
        return {'x': jax.random.normal(ks[0], (B, L, D), dtype=jnp.float32), 'Wq': jax.random.normal(ks[1], (D, D), dtype=jnp.float32) * s, 'bq': jnp.zeros((D,), dtype=jnp.float32), 'Wk': jax.random.normal(ks[2], (D, D), dtype=jnp.float32) * s, 'bk': jnp.zeros((D,), dtype=jnp.float32), 'Wv': jax.random.normal(ks[3], (D, D), dtype=jnp.float32) * s, 'bv': jnp.zeros((D,), dtype=jnp.float32), 'Wo': jax.random.normal(ks[4], (D, D), dtype=jnp.float32) * s, 'bo': jnp.zeros((D,), dtype=jnp.float32), 'gamma': jnp.ones((D,), dtype=jnp.float32), 'beta': jnp.zeros((D,), dtype=jnp.float32)}
    _L0_attn_all = _L0_attn_setup()
    _L0_attn_in = {k: v for k, v in _L0_attn_all.items() if k in ('Wq', 'bq', 'Wk', 'bk', 'Wv', 'bv', 'Wo', 'bo', 'gamma', 'beta')}
    del _L0_attn_all

    def _L0_ffn_setup():
        import jax, jax.numpy as jnp
        import numpy as np
        D_IN, D_HID, E, K = (128, 512, 10, 2)
        KS = (9, 1)

        def conv1d_same(x, w, b):
            y = jax.lax.conv_general_dilated(x, w, window_strides=(1,), padding='SAME', dimension_numbers=('NCH', 'OIH', 'NCH'))
            return y + b[None, :, None]
        key = jax.random.key(seed)
        ks = jax.random.split(key, 16)
        s = 0.02
        B, T = (2, 512)
        return {'x': jax.random.normal(ks[0], (B, T, D_IN), jnp.float32), 'rc_w1': jax.random.normal(ks[1], (D_IN, D_IN, 3), jnp.float32) * s, 'rc_b1': jnp.zeros((D_IN,), jnp.float32), 'rc_w2': jax.random.normal(ks[2], (E, D_IN, 3), jnp.float32) * s, 'rc_b2': jnp.zeros((E,), jnp.float32), 'sh_w1': jax.random.normal(ks[3], (D_HID, D_IN, KS[0]), jnp.float32) * s, 'sh_b1': jnp.zeros((D_HID,), jnp.float32), 'sh_w2': jax.random.normal(ks[4], (D_IN, D_HID, KS[1]), jnp.float32) * s, 'sh_b2': jnp.zeros((D_IN,), jnp.float32), 'e_w1': jax.random.normal(ks[5], (E, D_IN, D_HID), jnp.float32) * s, 'e_b1': jnp.zeros((E, D_HID), jnp.float32), 'e_w2': jax.random.normal(ks[6], (E, D_HID, D_IN), jnp.float32) * s, 'e_b2': jnp.zeros((E, D_IN), jnp.float32), 'ln_g': jnp.ones((D_IN,), jnp.float32), 'ln_b': jnp.zeros((D_IN,), jnp.float32)}
    _L0_ffn_all = _L0_ffn_setup()
    _L0_ffn_in = {k: v for k, v in _L0_ffn_all.items() if k in ('rc_w1', 'rc_b1', 'rc_w2', 'rc_b2', 'sh_w1', 'sh_b1', 'sh_w2', 'sh_b2', 'e_w1', 'e_b1', 'e_w2', 'e_b2', 'ln_g', 'ln_b')}
    del _L0_ffn_all
    return {'x': x, 'L0_tok_W': _L0_tok_in['W'], 'L0_tok_b': _L0_tok_in['b'], 'L0_attn_Wq': _L0_attn_in['Wq'], 'L0_attn_bq': _L0_attn_in['bq'], 'L0_attn_Wk': _L0_attn_in['Wk'], 'L0_attn_bk': _L0_attn_in['bk'], 'L0_attn_Wv': _L0_attn_in['Wv'], 'L0_attn_bv': _L0_attn_in['bv'], 'L0_attn_Wo': _L0_attn_in['Wo'], 'L0_attn_bo': _L0_attn_in['bo'], 'L0_attn_gamma': _L0_attn_in['gamma'], 'L0_attn_beta': _L0_attn_in['beta'], 'L0_ffn_rc_w1': _L0_ffn_in['rc_w1'], 'L0_ffn_rc_b1': _L0_ffn_in['rc_b1'], 'L0_ffn_rc_w2': _L0_ffn_in['rc_w2'], 'L0_ffn_rc_b2': _L0_ffn_in['rc_b2'], 'L0_ffn_sh_w1': _L0_ffn_in['sh_w1'], 'L0_ffn_sh_b1': _L0_ffn_in['sh_b1'], 'L0_ffn_sh_w2': _L0_ffn_in['sh_w2'], 'L0_ffn_sh_b2': _L0_ffn_in['sh_b2'], 'L0_ffn_e_w1': _L0_ffn_in['e_w1'], 'L0_ffn_e_b1': _L0_ffn_in['e_b1'], 'L0_ffn_e_w2': _L0_ffn_in['e_w2'], 'L0_ffn_e_b2': _L0_ffn_in['e_b2'], 'L0_ffn_ln_g': _L0_ffn_in['ln_g'], 'L0_ffn_ln_b': _L0_ffn_in['ln_b']}

def reference(x, L0_tok_W, L0_tok_b, L0_attn_Wq, L0_attn_bq, L0_attn_Wk, L0_attn_bk, L0_attn_Wv, L0_attn_bv, L0_attn_Wo, L0_attn_bo, L0_attn_gamma, L0_attn_beta, L0_ffn_rc_w1, L0_ffn_rc_b1, L0_ffn_rc_w2, L0_ffn_rc_b2, L0_ffn_sh_w1, L0_ffn_sh_b1, L0_ffn_sh_w2, L0_ffn_sh_b2, L0_ffn_e_w1, L0_ffn_e_b1, L0_ffn_e_w2, L0_ffn_e_b2, L0_ffn_ln_g, L0_ffn_ln_b):
    import jax
    import jax.numpy as jnp

    def _L0_tok_ref(x, W, b):
        import jax, jax.numpy as jnp
        import numpy as np
        PATCH_LEN = 16
        STRIDE = 8
        IN_FEATS = 32
        D_MODEL = 128
        B, L, F = x.shape
        num_patches = 1 + (L - PATCH_LEN) // STRIDE
        idx = jnp.arange(num_patches)[:, None] * STRIDE + jnp.arange(PATCH_LEN)[None, :]
        patches = x[:, idx, :]
        P = patches.reshape(B, num_patches, PATCH_LEN * F)
        return jnp.einsum('bnk,dk->bnd', P, W) + b

    def _L0_attn_ref(x, Wq, bq, Wk, bk, Wv, bv, Wo, bo, gamma, beta):
        import jax, jax.numpy as jnp
        import numpy as np
        NUM_HEAD = 8
        DIM_MODEL = 128
        DIM_HEAD = DIM_MODEL // NUM_HEAD
        LN_EPS = 1e-05
        B, L, D = x.shape
        H, dh = (NUM_HEAD, D // NUM_HEAD)
        Q = x @ Wq.T + bq
        K = x @ Wk.T + bk
        V = x @ Wv.T + bv
        Q = Q.reshape(B * H, L, dh)
        K = K.reshape(B * H, L, dh)
        V = V.reshape(B * H, L, dh)
        scale = dh ** (-0.5)
        attn = jax.nn.softmax(jnp.einsum('bqd,bkd->bqk', Q, K) * scale, axis=-1)
        context = jnp.einsum('bqk,bkd->bqd', attn, V)
        context = context.reshape(B, L, D)
        out = context @ Wo.T + bo
        out = out + x
        mu = jnp.mean(out, axis=-1, keepdims=True)
        var = jnp.mean(jnp.square(out - mu), axis=-1, keepdims=True)
        out = (out - mu) / jnp.sqrt(var + LN_EPS) * gamma + beta
        return out

    def _L0_ffn_ref(x, rc_w1, rc_b1, rc_w2, rc_b2, sh_w1, sh_b1, sh_w2, sh_b2, e_w1, e_b1, e_w2, e_b2, ln_g, ln_b):
        import jax, jax.numpy as jnp
        import numpy as np
        D_IN, D_HID, E, K = (128, 512, 10, 2)
        KS = (9, 1)

        def conv1d_same(x, w, b):
            y = jax.lax.conv_general_dilated(x, w, window_strides=(1,), padding='SAME', dimension_numbers=('NCH', 'OIH', 'NCH'))
            return y + b[None, :, None]
        B, T, d = x.shape
        residual = x
        xt = jnp.transpose(x, (0, 2, 1))
        rc = conv1d_same(xt, rc_w1, rc_b1)
        rc = jax.nn.gelu(rc, approximate=False)
        rc = conv1d_same(rc, rc_w2, rc_b2)
        logits = jnp.transpose(rc, (0, 2, 1)).reshape(-1, E)
        vals, idx = jax.lax.top_k(logits, K)
        gv = jax.nn.softmax(vals, axis=-1)
        N = logits.shape[0]
        gates = jnp.zeros((N, E), x.dtype).at[jnp.arange(N)[:, None], idx].set(gv)
        x2 = x.reshape(-1, d)
        h = jnp.einsum('nd,edh->enh', x2, e_w1) + e_b1[:, None, :]
        h = jax.nn.elu(h)
        eo = jnp.einsum('enh,ehd->end', h, e_w2) + e_b2[:, None, :]
        y = jnp.einsum('end,ne->nd', eo, gates).reshape(B, T, d)
        sh = conv1d_same(xt, sh_w1, sh_b1)
        sh = jax.nn.silu(sh)
        sh = conv1d_same(sh, sh_w2, sh_b2)
        sh = jnp.transpose(sh, (0, 2, 1))
        z = residual + y + sh
        mu = jnp.mean(z, axis=-1, keepdims=True)
        var = jnp.mean(jnp.square(z - mu), axis=-1, keepdims=True)
        return (z - mu) * jax.lax.rsqrt(var + 1e-05) * ln_g + ln_b
    h = _L0_tok_ref(x, L0_tok_W, L0_tok_b)
    h = h + _L0_attn_ref(_layernorm(h, axis=-1), L0_attn_Wq, L0_attn_bq, L0_attn_Wk, L0_attn_bk, L0_attn_Wv, L0_attn_bv, L0_attn_Wo, L0_attn_bo, L0_attn_gamma, L0_attn_beta)
    h = h + _L0_ffn_ref(_layernorm(h, axis=-1), L0_ffn_rc_w1, L0_ffn_rc_b1, L0_ffn_rc_w2, L0_ffn_rc_b2, L0_ffn_sh_w1, L0_ffn_sh_b1, L0_ffn_sh_w2, L0_ffn_sh_b2, L0_ffn_e_w1, L0_ffn_e_b1, L0_ffn_e_w2, L0_ffn_e_b2, L0_ffn_ln_g, L0_ffn_ln_b)
    return h

_drawn_inputs = setup_inputs


def setup_inputs(seed=0):
    import zlib

    import numpy as np

    out = dict(_drawn_inputs(seed))
    spreads = {'L0_attn_bq': (0.0, 0.8),
     'L0_attn_bk': (0.0, 0.8),
     'L0_attn_bv': (0.0, 0.8),
     'L0_attn_bo': (0.0, 0.1),
     'L0_attn_gamma': (1.0, 0.2),
     'L0_attn_beta': (0.0, 0.1),
     'L0_ffn_rc_b1': (0.0, 0.46),
     'L0_ffn_rc_b2': (0.0, 0.1),
     'L0_ffn_sh_b1': (0.0, 0.763),
     'L0_ffn_sh_b2': (0.0, 0.1),
     'L0_ffn_e_b1': (0.0, 0.719),
     'L0_ffn_e_b2': (0.0, 0.302),
     'L0_ffn_ln_g': (1.0, 0.2),
     'L0_ffn_ln_b': (0.0, 0.1)}
    factors = {'L0_attn_Wq': 8.0, 'L0_attn_Wk': 8.0, 'L0_attn_Wv': 6.325, 'L0_attn_Wo': 5.605}
    for name, (base, spread) in spreads.items():
        noise = np.random.default_rng([zlib.crc32(name.encode()), seed]).standard_normal(out[name].shape)
        drawn = base * np.exp(spread * noise) if base else spread * noise
        out[name] = jnp.asarray(drawn.astype(out[name].dtype))
    for name, factor in factors.items():
        out[name] = (out[name] * factor).astype(out[name].dtype)
    return out
```

```python
from contextlib import ExitStack

import numpy as np

import concourse.bass as bass
from concourse import mybir

F32 = mybir.dt.float32
ALU = mybir.AluOpType
ACT = mybir.ActivationFunctionType
AX = mybir.AxisListType

P = 128
B, LX, FEATS = 64, 125, 32
STRIDE, PATCH = 8, 16
T = 1 + (LX - PATCH) // STRIDE
N = B * T
NT = N // P
D = 128
KP = PATCH * FEATS // P
JX = 2 * (T - 1) + KP
H, DH = 8, 16
R = H * T
EPS = 1e-5
NEG = -1e30
E, DHID = 10, 512
HC = DHID // P
KSH, KRC = 9, 3
HALVES = [(0, 512), (512, N)]
TILES = [range(0, 4), range(4, NT)]
G4 = 4
NG = B // G4
GV = 16

C_BQ, C_BK, C_BV, C_RC1, C_RC2 = 0, 1, 2, 3, 4
C_SH1 = 5
C_E1 = C_SH1 + HC
C_N = C_E1 + E * HC
R_TOK, R_BO, R_GAMMA, R_BETA, R_SH2, R_LNG, R_LNB = range(7)


def conv_pieces(taps, half):
    lo, hi = HALVES[half]
    mid = taps // 2
    out = []
    for tap in [mid] + [k for k in range(taps) if k != mid]:
        d = (tap - mid) * B
        a, b = max(lo, -d), min(hi, N - d)
        if a < b:
            out.append((tap, a, b, a + d))
    return out


def build(nc, xT, wtok, wqkvo, wrc1, wrc2, wsh1, wsh2, we1, we2, eb2, cols, rows, qmask, kmask, ident, tri, nsel, out):
    with ExitStack() as ctx:
        def sb(name, shape, dt=F32):
            return ctx.enter_context(nc.sbuf_tensor(name, shape, dt))

        def sem(name):
            return ctx.enter_context(nc.semaphore(name))

        xT_s = sb("xT_s", [P, 2, JX // 2, B])
        wtok_s = sb("wtok_s", [P, KP, D])
        wqkvo_s = sb("wqkvo_s", [P, 4, D])
        wrc1_s = sb("wrc1_s", [P, KRC, D])
        wrc2_s = sb("wrc2_s", [P, KRC, E])
        wsh1_s = sb("wsh1_s", [P, KSH, DHID])
        wsh2_s = sb("wsh2_s", [P, HC, D])
        we1_s = sb("we1_s", [P, E, DHID])
        we2_s = sb("we2_s", [P, E, HC, D])
        eb2_s = sb("eb2_s", [E, D])
        cols_s = sb("cols_s", [P, C_N])
        rows_s = sb("rows_s", [P, 7, D])
        ident_s = sb("ident_s", [P, P])
        tri_s = sb("tri_s", [P, E, E])
        nsel_s = sb("nsel_s", [P, E, E])

        h = sb("h", [P, NT, D])
        x1 = sb("x1", [P, NT, D])
        x1bo = sb("x1bo", [P, NT, D])
        hbeta = sb("hbeta", [P, NT, D])
        xnT = sb("xnT", [P, N])
        qkvT = sb("qkvT", [P, 3, N])
        QRm = sb("QRm", [P, R * B])
        KRm = sb("KRm", [P, R * B])
        QR = QRm[0:DH + H, :].rearrange("p (r b) -> p r b", b=B)
        KR = KRm[0:DH + H, :].rearrange("p (r b) -> p r b", b=B)
        VR = sb("VR", [R, DH + 1, B])
        mx = sb("mx", [R, B])
        nmxT = sb("nmxT", [B, R])
        ET = sb("ET", [R, 4, G4, R])
        rden = sb("rden", [R, B])
        CR = sb("CR", [R, DH, B])
        cT = sb("cT", [P, N])
        o = sb("o", [P, NT, D])
        on = x1
        h2 = sb("h2", [P, NT, D])
        spare = xT_s[:].rearrange("p a j b -> p (a j b)")
        x3 = spare[:, 0:NT * D].rearrange("p (i d) -> p i d", d=D)
        z = spare[:, NT * D:2 * NT * D].rearrange("p (i d) -> p i d", d=D)
        stats = sb("stats", [P, 4, NT, 6])
        mv = sb("mv", [P, 4, NT, 2])
        veps = sb("veps", [P, 4, NT])
        rstd = sb("rstd", [P, 4, NT])
        mhalf = sb("mhalf", [P, NT])
        rT = cT
        LT = sb("LT", [E, N])
        L = sb("L", [P, NT, E])
        m1 = sb("m1", [P, NT])
        Ld = sb("Ld", [P, NT, E])
        Lx = sb("Lx", [P, NT, E])
        rank = sb("rank", [P, NT, E])
        gates = sb("gates", [P, NT, E])
        den = sb("den", [P, NT])
        gatesT = sb("gatesT", [E, N])
        cols1 = sb("cols1", [P, E * HC])
        eb2c = sb("eb2c", [E, D])
        shT = QRm[:, 0:HC * N].rearrange("p (c n) -> p c n", c=HC)
        mn = QRm[:, HC * N:HC * N + 1024].rearrange("p (k n) -> p k n", k=2)
        ex = QRm[:, HC * N + 1024:HC * N + 2048].rearrange("p (k n) -> p k n", k=2)
        hid = KRm[:, 0:2 * HC * 512].rearrange("p (k c n) -> p k c n", k=2, c=HC)
        gt = KRm[:, 4096:4096 + NT * E * E].rearrange("p (i e f) -> p i e f", i=NT, e=E)
        eq = KRm[:, 4096 + NT * E * E:4096 + 2 * NT * E * E].rearrange("p (i e f) -> p i e f", i=NT, e=E)

        v_dram = nc.dram_tensor("v_rows", (D, N), F32, kind="Internal").ap()
        c_dram = nc.dram_tensor("c_rows", (D, N), F32, kind="Internal").ap()
        ps = [ctx.enter_context(nc.psum_tensor(f"bank{i}", [P, 512], F32)) for i in range(8)]

        ld = {k: sem("ld_" + k) for k in ("x", "tok", "cst", "qkvo", "mask", "rc", "sh", "e")}
        q = {}

        def S(name):
            if name not in q:
                q[name] = sem(name)
            return q[name]

        block = ctx.enter_context(nc.Block())
        NLN = 7

        @block.sync
        def _(sp):
            sp.dma_start(xT_s[:], xT).then_inc(ld["x"], 16)
            sp.dma_start(wtok_s[:], wtok).then_inc(ld["tok"], 16)
            sp.dma_start(rows_s[:], rows.partition_broadcast(P) if False else rows).then_inc(ld["cst"], 16)
            sp.dma_start(cols_s[:], cols).then_inc(ld["cst"], 16)
            sp.dma_start(ident_s[:], ident).then_inc(ld["cst"], 16)
            sp.dma_start(tri_s[:], tri).then_inc(ld["cst"], 16)
            sp.dma_start(nsel_s[:], nsel).then_inc(ld["cst"], 16)
            sp.dma_start(eb2_s[:], eb2).then_inc(ld["cst"], 16)
            sp.dma_start(wqkvo_s[:], wqkvo).then_inc(ld["qkvo"], 16)
            sp.dma_start(QR[DH:DH + H], qmask).then_inc(ld["mask"], 16)
            sp.dma_start(KR[DH:DH + H], kmask).then_inc(ld["mask"], 16)
            for n, dst in ((0, QR), (1, KR)):
                sp.wait_ge(S("qkv_done"), 2 * (n + 1))
                for c in range(H):
                    sp.dma_start(dst[0:DH, c * T:(c + 1) * T, :], qkvT[c * DH:(c + 1) * DH, n, :]
                                 .rearrange("p (l b) -> p l b", b=B)).then_inc(S("rows_in"), 16)
            sp.wait_ge(S("qkv_done"), 6)
            sp.dma_start(v_dram, qkvT[:, 2, :]).then_inc(S("v_out"), 16)
            sp.wait_ge(S("v_out"), 16)
            for c in range(H):
                sp.dma_start(VR[c * T:(c + 1) * T, 0:DH, :],
                             v_dram[c * DH:(c + 1) * DH, :].rearrange("e (l b) -> l e b", b=B)).then_inc(S("v_in"), 16)
            sp.wait_ge(S("ctx_done"), B // GV)
            for c in range(H):
                sp.dma_start(c_dram[c * DH:(c + 1) * DH, :].rearrange("e (l b) -> l e b", b=B),
                             CR[c * T:(c + 1) * T, :, :]).then_inc(S("c_out"), 16)
            sp.wait_ge(S("c_out"), 16 * H)
            sp.dma_start(cT[:], c_dram).then_inc(S("c_in"), 16)
            for i in range(NT):
                sp.wait_ge(S("out_done"), i + 1)
                sp.dma_start(out[:, 2 * i:2 * i + 2, :].rearrange("b t d -> t b d"), z[:, i, :]).then_inc(S("stored"), 16)
            sp.wait_ge(S("stored"), 16 * NT)

        @block.gpsimd
        def _(pool):
            pool.dma_start(wrc1_s[:], wrc1).then_inc(ld["rc"], 16)
            pool.dma_start(wrc2_s[:], wrc2).then_inc(ld["rc"], 16)
            pool.dma_start(wsh1_s[:], wsh1).then_inc(ld["sh"], 16)
            pool.dma_start(wsh2_s[:], wsh2).then_inc(ld["sh"], 16)
            pool.dma_start(we1_s[:], we1).then_inc(ld["e"], 16)
            pool.dma_start(we2_s[:], we2).then_inc(ld["e"], 16)
            pool.memset(mhalf[:], -0.5).then_inc(S("mhalf"), 1)
            pool.memset(VR[:, DH:DH + 1, :], 1.0).then_inc(S("ones_in"), 1)
            pool.wait_ge(S("mhalf"), 1)

            def inv_std(n):
                pool.wait_ge(S("var_done"), n + 1)
                pool.tensor_tensor(rstd[:, n, :], veps[:, n, :], mhalf[:], ALU.pow).then_inc(S("rstd_done"), 1)

            inv_std(0)
            pool.wait_ge(S("x1_done"), NT)
            pool.wait_ge(ld["cst"], 96)
            for i in range(NT):
                pool.tensor_tensor(x1bo[:, i, :], x1[:, i, :], rows_s[:, R_BO, :], ALU.add).then_inc(S("x1bo_done"), 1)
                pool.tensor_tensor(hbeta[:, i, :], h[:, i, :], rows_s[:, R_BETA, :], ALU.add).then_inc(S("hbeta_done"), 1)
            for n in (1, 2, 3):
                inv_std(n)

        @block.tensor
        def _(pe):
            mm = nc.tensor.matmul
            pe.wait_ge(ld["x"], 16)
            pe.wait_ge(ld["tok"], 16)
            for hf in range(2):
                for i in TILES[hf]:
                    col = (i - TILES[hf][0]) * D
                    for k in range(KP):
                        a = 2 * i + k // 2
                        ins = mm(ps[hf][:, col:col + D], xT_s[:, k % 2, a:a + 2, :], wtok_s[:, k, :],
                                 start=(k == 0), stop=(k == KP - 1))
                ins.then_inc(S("tok_mm"), 1)
            pe.wait_ge(ld["e"], 32)
            pe.wait_ge(ld["cst"], 96)
            for e in range(E):
                for c in range(HC):
                    ins = mm(ps[7][0:E, 0:D], nsel_s[:, e, :], we2_s[:, e, c, :],
                             start=(e == 0 and c == 0), stop=(e == E - 1 and c == HC - 1))
            ins.then_inc(S("colsum_mm"), 1)

            def transposes(src, done, banks, tag):
                for hf in range(2):
                    pe.wait_ge(S(done), TILES[hf][-1] + 1)
                    for i in TILES[hf]:
                        col = (i - TILES[hf][0]) * P
                        ins = nc.tensor.transpose(ps[banks[hf]][:, col:col + P], src[:, i, :], ident_s[:])
                    ins.then_inc(S(tag), 1)

            transposes(x1, "x1_done", (2, 3), "x1T_mm")
            pe.wait_ge(ld["qkvo"], 16)
            for n in range(3):
                for hf, (lo, hi) in enumerate(HALVES):
                    pe.wait_ge(S("x1T_done"), hf + 1)
                    bank = (4, 5, 6, 0, 1, 2)[2 * n + hf]
                    mm(ps[bank][:, 0:hi - lo], wqkvo_s[:, n, :], xnT[:, lo:hi], start=True, stop=True).then_inc(S("qkv_mm"), 1)
            pe.wait_ge(S("rows_in"), 16 * 2 * H)
            pe.wait_ge(ld["mask"], 32)
            pe.wait_ge(S("qkv_done"), 6)
            pe.wait_ge(S("eb2c_done"), 1)
            for g in range(NG):
                if g >= 4:
                    pe.wait_ge(S("mx_done"), g - 3)
                for j in range(G4):
                    b = g * G4 + j
                    ins = mm(ps[g % 4][0:R, j * R:(j + 1) * R], QR[:, :, b], KR[:, :, b], start=True, stop=True)
                ins.then_inc(S("s_mm"), 1)
            pe.wait_ge(S("mx_done"), NG)
            nc.tensor.transpose(ps[4][0:B, 0:R], mx[:, :], ident_s[0:R, 0:R]).then_inc(S("mxT_mm"), 1)
            pe.wait_ge(S("nmxT_done"), 1)

            def scores_t(g):
                if g >= 4:
                    pe.wait_ge(S("exp_done"), g - 3)
                for j in range(G4):
                    b = g * G4 + j
                    mm(ps[g % 4][0:R, j * R:(j + 1) * R], KR[:, :, b], QR[:, :, b], start=True, stop=False)
                    ins = mm(ps[g % 4][0:R, j * R:(j + 1) * R], ident_s[0:B, b:b + 1].broadcast_to([B, R]), nmxT[:, :],
                             start=False, stop=True)
                ins.then_inc(S("st_mm"), 1)

            def context(g):
                pe.wait_ge(S("exp_done"), g + 1)
                for j in range(G4):
                    b = g * G4 + j
                    col = (b % GV) * (DH + 1)
                    ins = mm(ps[4 + b // GV][0:R, col:col + DH + 1], ET[:, g % 4, j, :], VR[:, :, b], start=True, stop=True)
                ins.then_inc(S("ctx_mm"), 1)

            pe.wait_ge(S("v_in"), 16 * H)
            pe.wait_ge(S("ones_in"), 1)
            for g in range(NG):
                scores_t(g)
                if g:
                    context(g - 1)
            context(NG - 1)
            pe.wait_ge(S("c_in"), 16)
            for hf in range(2):
                for i in TILES[hf]:
                    col = (i - TILES[hf][0]) * D
                    ins = mm(ps[hf][:, col:col + D], cT[:, i * P:(i + 1) * P], wqkvo_s[:, 3, :], start=True, stop=True)
                ins.then_inc(S("o_mm"), 1)
            transposes(x3, "x3_done", (2, 3), "x3T_mm")

            def conv(bank, hf, w, taps, M):
                lo, _ = HALVES[hf]
                pieces = conv_pieces(taps, hf)
                for n, (tap, a, b, src) in enumerate(pieces):
                    ins = mm(ps[bank][0:M, a - lo:b - lo], w(tap), (xnT if M == D else rT)[:, src:src + b - a],
                             start=(n == 0), stop=(n == len(pieces) - 1))
                return ins

            pe.wait_ge(ld["rc"], 32)
            pe.wait_ge(S("x3T_done"), 2)
            for hf in range(2):
                conv(4 + hf, hf, lambda k: wrc1_s[:, k, :], KRC, D).then_inc(S("rc1_mm"), 1)
            pe.wait_ge(S("gelu_done"), 2)
            for hf in range(2):
                conv(6 + hf, hf, lambda k: wrc2_s[:, k, :], KRC, E).then_inc(S("rc2_mm"), 1)
            pe.wait_ge(S("LT_done"), 2)
            for i in range(NT):
                ins = nc.tensor.transpose(ps[0][:, i * E:(i + 1) * E], LT[:, i * P:(i + 1) * P], ident_s[0:E, 0:E])
            ins.then_inc(S("L_mm"), 1)
            pe.wait_ge(ld["sh"], 32)
            for n in range(2 * HC):
                c, hf = n // 2, n % 2
                if n >= 2:
                    pe.wait_ge(S("silu_done"), n - 1)
                conv(4 + n % 2, hf, lambda k: wsh1_s[:, k, c * P:(c + 1) * P], KSH, D).then_inc(S("sh1_mm"), 1)
            pe.wait_ge(S("gates_done"), 1)
            for hf in range(2):
                for i in TILES[hf]:
                    col = (i - TILES[hf][0]) * P
                    ins = nc.tensor.transpose(ps[6 + hf][0:E, col:col + P], gates[:, i, :], ident_s[:])
                ins.then_inc(S("gT_mm"), 1)
            pe.wait_ge(S("silu_done"), 2 * HC)
            pe.wait_ge(S("gT_done"), 2)
            for hf in range(2):
                for i in TILES[hf]:
                    o_ap = ps[hf][:, (i - TILES[hf][0]) * D:(i - TILES[hf][0] + 1) * D]
                    for c in range(HC):
                        mm(o_ap, shT[:, c, i * P:(i + 1) * P], wsh2_s[:, c, :], start=(c == 0), stop=False)
                    ins = mm(o_ap, gatesT[:, i * P:(i + 1) * P], eb2c[:, :], start=False, stop=True)
                ins.then_inc(S("sh2_mm"), 1)

            def up(u):
                e, hf = u // 2, u % 2
                lo, hi = HALVES[hf]
                for c in range(HC):
                    k = u * HC + c
                    if k >= 4:
                        pe.wait_ge(S("hid_done"), k - 3)
                    else:
                        pe.wait_ge(S("z0_done"), 2)
                    mm(ps[2 + k % 4][:, 0:hi - lo], we1_s[:, e, c * P:(c + 1) * P], xnT[:, lo:hi],
                       start=True, stop=True).then_inc(S("up_mm"), 1)

            def down(u):
                e, hf = u // 2, u % 2
                pe.wait_ge(S("hid_done"), (u + 1) * HC)
                if u >= 2:
                    pe.wait_ge(S("y_done"), u - 1)
                for i in TILES[hf]:
                    j = i - TILES[hf][0]
                    for c in range(HC):
                        ins = mm(ps[6 + u % 2][:, j * D:(j + 1) * D], hid[:, u % 2, c, j * P:(j + 1) * P],
                                 we2_s[:, e, c, :], start=(c == 0), stop=(c == HC - 1))
                ins.then_inc(S("down_mm"), 1)

            for u in range(2 * E):
                up(u)
                if u:
                    down(u - 1)
            down(2 * E - 1)

        @block.scalar
        def _(act):
            A = nc.scalar.activation
            for hf, (lo, hi) in enumerate(HALVES):
                act.wait_ge(S("x1T_mm"), hf + 1)
                A(xnT[:, lo:hi], ps[2 + hf][:, 0:hi - lo], ACT.Copy).then_inc(S("x1T_done"), 1)
            for n in range(3):
                for hf, (lo, hi) in enumerate(HALVES):
                    bank = (4, 5, 6, 0, 1, 2)[2 * n + hf]
                    act.wait_ge(S("qkv_mm"), 2 * n + hf + 1)
                    A(qkvT[:, n, lo:hi], ps[bank][:, 0:hi - lo], ACT.Identity,
                      bias=cols_s[:, C_BQ + n:C_BQ + n + 1]).then_inc(S("qkv_done"), 1)
            for g in range(NG):
                act.wait_ge(S("st_mm"), g + 1)
                if g >= 4:
                    act.wait_ge(S("ctx_mm"), g - 3)
                A(ET[:, g % 4, :, :], ps[g % 4][0:R, 0:G4 * R].rearrange("p (j r) -> p j r", j=G4), ACT.Exp,
                  scale=float(DH) ** -0.5).then_inc(S("exp_done"), 1)
            for hf, (lo, hi) in enumerate(HALVES):
                act.wait_ge(S("x3T_mm"), hf + 1)
                A(xnT[:, lo:hi], ps[2 + hf][:, 0:hi - lo], ACT.Copy).then_inc(S("x3T_done"), 1)
            for hf, (lo, hi) in enumerate(HALVES):
                act.wait_ge(S("rc1_mm"), hf + 1)
                A(rT[:, lo:hi], ps[4 + hf][:, 0:hi - lo], ACT.Gelu, bias=cols_s[:, C_RC1:C_RC1 + 1]).then_inc(S("gelu_done"), 1)
            for hf, (lo, hi) in enumerate(HALVES):
                act.wait_ge(S("rc2_mm"), hf + 1)
                A(LT[:, lo:hi], ps[6 + hf][0:E, 0:hi - lo], ACT.Identity,
                  bias=cols_s[0:E, C_RC2:C_RC2 + 1]).then_inc(S("LT_done"), 1)
            for n in range(2 * HC):
                c, hf = n // 2, n % 2
                lo, hi = HALVES[hf]
                act.wait_ge(S("sh1_mm"), n + 1)
                A(shT[:, c, lo:hi], ps[4 + n % 2][:, 0:hi - lo], ACT.Silu,
                  bias=cols_s[:, C_SH1 + c:C_SH1 + c + 1]).then_inc(S("silu_done"), 1)
                if n == 1:
                    act.wait_ge(S("Ld_done"), 1)
                    A(Lx[:], Ld[:], ACT.Exp).then_inc(S("Lx_done"), 1)
            for k in range(2 * E * HC):
                lo, hi = HALVES[k // HC % 2]
                act.wait_ge(S("mn_done"), k + 1)
                if k >= 2:
                    act.wait_ge(S("hid_done"), k - 1)
                A(ex[:, k % 2, 0:hi - lo], mn[:, k % 2, 0:hi - lo], ACT.Exp).then_inc(S("ex_done"), 1)

        @block.vector
        def _(dve):
            V = nc.vector
            chain = [0]

            def link(ins):
                chain[0] += 1
                ins.then_inc(S("dve_chain"), 1)
                dve.wait_ge(S("dve_chain"), chain[0])

            def bc(row):
                return rows_s[:, row:row + 1, :]

            def layernorm_stats(n, src):
                for i in range(NT):
                    ins = V.bn_stats(stats[:, n, i, :], src[:, i, :])
                link(ins)
                for i in range(NT):
                    ins = V.bn_aggr(mv[:, n, i, :], stats[:, n, i, :])
                link(ins)
                V.tensor_scalar(veps[:, n, :], mv[:, n, :, 1], EPS, None, ALU.add).then_inc(S("var_done"), 1)
                dve.wait_ge(S("rstd_done"), n + 1)

            def normalise(n, dst, src, tag):
                for i in range(NT):
                    V.tensor_scalar(dst[:, i, :], src[:, i, :], mv[:, n, i, 0:1], rstd[:, n, i:i + 1],
                                    ALU.subtract, ALU.mult).then_inc(S(tag), 1)

            dve.wait_ge(ld["cst"], 96)
            link(V.tensor_scalar(cols1[:], cols_s[:, C_E1:C_E1 + E * HC], 1.0, None, ALU.add))
            for hf in range(2):
                dve.wait_ge(S("tok_mm"), hf + 1)
                n = len(TILES[hf])
                i0 = TILES[hf][0]
                link(V.tensor_tensor(h[:, i0:i0 + n, :], ps[hf][:, 0:n * D].rearrange("p (i d) -> p i d", d=D),
                                     bc(R_TOK).broadcast_to([P, n, D]), ALU.add))
            layernorm_stats(0, h)
            normalise(0, x1, h, "x1_done")
            dve.wait_ge(S("colsum_mm"), 1)
            V.tensor_tensor(eb2c[:], ps[7][0:E, 0:D], eb2_s[:], ALU.add).then_inc(S("eb2c_done"), 1)
            for g in range(NG):
                dve.wait_ge(S("s_mm"), g + 1)
                V.tensor_reduce(mx[:, g * G4:(g + 1) * G4], ps[g % 4][0:R, 0:G4 * R].rearrange("p (j s) -> p j s", j=G4),
                                AX.X, ALU.max).then_inc(S("mx_done"), 1)
            dve.wait_ge(S("mxT_mm"), 1)
            V.tensor_scalar(nmxT[:], ps[4][0:B, 0:R], -1.0, None, ALU.mult).then_inc(S("nmxT_done"), 1)
            for g in range(B // GV):
                dve.wait_ge(S("ctx_mm"), (g + 1) * GV // G4)
                acc = ps[4 + g][0:R, 0:GV * (DH + 1)].rearrange("p (b e) -> p b e", e=DH + 1)
                rd = rden[:, g * GV:(g + 1) * GV]
                link(V.reciprocal(rd, acc[:, :, DH]))
                V.tensor_tensor(CR[:, :, g * GV:(g + 1) * GV].rearrange("p e b -> p b e"), acc[:, :, 0:DH],
                                rd.rearrange("p (b o) -> p b o", o=1).broadcast_to([R, GV, DH]),
                                ALU.mult).then_inc(S("ctx_done"), 1)
            for hf in range(2):
                dve.wait_ge(S("o_mm"), hf + 1)
                dve.wait_ge(S("x1bo_done"), NT)
                n = len(TILES[hf])
                i0 = TILES[hf][0]
                link(V.tensor_tensor(o[:, i0:i0 + n, :], ps[hf][:, 0:n * D].rearrange("p (i d) -> p i d", d=D),
                                     x1bo[:, i0:i0 + n, :], ALU.add))
            layernorm_stats(1, o)
            normalise(1, on, o, "on_done")
            dve.wait_ge(S("on_done"), NT)
            dve.wait_ge(S("hbeta_done"), NT)
            link(V.tensor_tensor(on[:], on[:], bc(R_GAMMA).broadcast_to([P, NT, D]), ALU.mult))
            link(V.tensor_tensor(h2[:], on[:], hbeta[:], ALU.add))
            layernorm_stats(2, h2)
            normalise(2, x3, h2, "x3_done")
            dve.wait_ge(S("L_mm"), 1)
            link(V.tensor_copy(L[:], ps[0][:, 0:NT * E].rearrange("p (i e) -> p i e", e=E)))
            link(V.tensor_reduce(m1[:], L[:], AX.X, ALU.max))
            V.tensor_tensor(Ld[:], L[:], m1[:].rearrange("p (i o) -> p i o", o=1).broadcast_to([P, NT, E]),
                            ALU.subtract).then_inc(S("Ld_done"), 1)
            other = L[:].rearrange("p i (o f) -> p i o f", o=1).broadcast_to([P, NT, E, E])
            mine = L[:].rearrange("p i (e o) -> p i e o", o=1).broadcast_to([P, NT, E, E])
            V.tensor_tensor(gt, other, mine, ALU.is_gt)
            link(V.tensor_tensor(eq, other, mine, ALU.is_equal))
            link(V.tensor_tensor(eq, eq, tri_s[:].rearrange("p (o e) f -> p o e f", o=1).broadcast_to([P, NT, E, E]),
                                 ALU.mult))
            link(V.tensor_tensor(gt, gt, eq, ALU.add))
            link(V.tensor_reduce(rank[:], gt, AX.X, ALU.add))
            dve.wait_ge(S("Lx_done"), 1)
            link(V.scalar_tensor_tensor(gates[:], rank[:], 1.5, Lx[:], ALU.is_lt, ALU.mult))
            link(V.tensor_reduce(den[:], gates[:], AX.X, ALU.add))
            link(V.reciprocal(den[:], den[:]))
            V.tensor_tensor(gates[:], gates[:], den[:].rearrange("p (i o) -> p i o", o=1).broadcast_to([P, NT, E]),
                            ALU.mult).then_inc(S("gates_done"), 1)
            for hf, (lo, hi) in enumerate(HALVES):
                dve.wait_ge(S("gT_mm"), hf + 1)
                V.tensor_copy(gatesT[:, lo:hi], ps[6 + hf][0:E, 0:hi - lo]).then_inc(S("gT_done"), 1)
            link(V.tensor_tensor(z, x3, bc(R_SH2).broadcast_to([P, NT, D]), ALU.add))
            for hf in range(2):
                dve.wait_ge(S("sh2_mm"), hf + 1)
                n = len(TILES[hf])
                i0 = TILES[hf][0]
                V.tensor_tensor(z[:, i0:i0 + n, :], ps[hf][:, 0:n * D].rearrange("p (i d) -> p i d", d=D),
                                z[:, i0:i0 + n, :], ALU.add).then_inc(S("z0_done"), 1)
            dve.wait_ge(S("z0_done"), 2)

            def low(k):
                u, c = k // HC, k % HC
                lo, hi = HALVES[u % 2]
                dve.wait_ge(S("up_mm"), k + 1)
                if k >= 2:
                    dve.wait_ge(S("ex_done"), k - 1)
                V.tensor_scalar(mn[:, k % 2, 0:hi - lo], ps[2 + k % 4][:, 0:hi - lo],
                                cols_s[:, C_E1 + u // 2 * HC + c:C_E1 + u // 2 * HC + c + 1], 0.0,
                                ALU.add, ALU.min).then_inc(S("mn_done"), 1)

            def high(k):
                u, c = k // HC, k % HC
                lo, hi = HALVES[u % 2]
                dve.wait_ge(S("ex_done"), k + 1)
                if u >= 2:
                    dve.wait_ge(S("down_mm"), u - 1)
                n = u // 2 * HC + c
                V.scalar_tensor_tensor(hid[:, u % 2, c, 0:hi - lo], ps[2 + k % 4][:, 0:hi - lo], cols1[:, n:n + 1],
                                       ex[:, k % 2, 0:hi - lo], ALU.add, ALU.max).then_inc(S("hid_done"), 1)

            def gated(u):
                e, hf = u // 2, u % 2
                dve.wait_ge(S("down_mm"), u + 1)
                if u >= 2:
                    dve.wait_ge(S("y_done"), u - 1)
                for i in TILES[hf]:
                    j = i - TILES[hf][0]
                    ins = V.scalar_tensor_tensor(z[:, i, :], ps[6 + u % 2][:, j * D:(j + 1) * D], gates[:, i, e:e + 1],
                                                 z[:, i, :], ALU.mult, ALU.add)
                ins.then_inc(S("y_done"), 1)

            K = 2 * E * HC
            for k in range(K + 1):
                if k < K:
                    low(k)
                if k:
                    high(k - 1)
                if k >= 2 * HC and k % HC == 1:
                    gated(k // HC - 2)
            gated(2 * E - 2)
            gated(2 * E - 1)
            dve.wait_ge(S("y_done"), 2 * E)
            layernorm_stats(3, z)
            normalise(3, z, z, "zn_done")
            dve.wait_ge(S("zn_done"), NT)
            link(V.tensor_tensor(h2[:], h2[:], bc(R_LNB).broadcast_to([P, NT, D]), ALU.add))
            for i in range(NT):
                link(V.tensor_tensor(z[:, i, :], z[:, i, :], rows_s[:, R_LNG, :], ALU.mult))
                V.tensor_tensor(z[:, i, :], z[:, i, :], h2[:, i, :], ALU.add).then_inc(S("out_done"), 1)


def shape_constants():
    c, l = np.divmod(np.arange(R), T)
    head = (l * H + c) // T
    same = (np.arange(H)[:, None] == head[None, :]).astype(np.float32)
    q = np.ascontiguousarray(np.broadcast_to(same[:, :, None], (H, R, B)))
    k = np.ascontiguousarray(np.broadcast_to(np.where(same > 0, 0.0, NEG).astype(np.float32)[:, :, None], (H, R, B)))
    tri = np.ascontiguousarray(np.broadcast_to(np.tril(np.ones((E, E), np.float32), -1), (P, E, E)))
    nsel = np.ascontiguousarray(np.broadcast_to(-np.eye(E, dtype=np.float32), (P, E, E)))
    return q, k, np.eye(P, dtype=np.float32), tri, nsel


def kernel(**inputs):
    import numpy as _np
    import concourse.bacc as _bacc
    from concourse import mybir as _mybir
    from concourse.bass_utils import run_bass_kernel_spmd as _run

    a = {k: _np.asarray(v) for k, v in inputs.items()}
    f = lambda n: a["L0_ffn_" + n]
    at = lambda n: a["L0_attn_" + n]
    colv = _np.zeros((P, C_N), _np.float32)
    for n, name in ((C_BQ, "bq"), (C_BK, "bk"), (C_BV, "bv")):
        colv[:, n] = at(name)
    colv[:, C_RC1] = f("rc_b1")
    colv[:E, C_RC2] = f("rc_b2")
    colv[:, C_SH1:C_E1] = f("sh_b1").reshape(HC, P).T
    colv[:, C_E1:] = f("e_b1").reshape(E * HC, P).T
    rowv = _np.stack([a["L0_tok_b"], at("bo"), at("gamma"), at("beta"), f("sh_b2"), f("ln_g"), f("ln_b")])
    qmask, kmask, ident, tri, nsel = shape_constants()
    laid = {
        "xT": a["x"].reshape(B, LX * FEATS)[:, :JX * P].reshape(B, JX // 2, 2, P).transpose(3, 2, 1, 0),
        "wtok": a["L0_tok_W"].T.reshape(KP, P, D).transpose(1, 0, 2),
        "wqkvo": _np.stack([at("Wq").T, at("Wk").T, at("Wv").T, at("Wo").T], axis=1),
        "wrc1": f("rc_w1").transpose(1, 2, 0),
        "wrc2": f("rc_w2").transpose(1, 2, 0),
        "wsh1": f("sh_w1").transpose(1, 2, 0),
        "wsh2": f("sh_w2")[:, :, 0].T.reshape(HC, P, D).transpose(1, 0, 2),
        "we1": f("e_w1").transpose(1, 0, 2),
        "we2": f("e_w2").reshape(E, HC, P, D).transpose(2, 0, 1, 3),
        "eb2": f("e_b2"),
        "cols": colv,
        "rows": _np.broadcast_to(rowv[None], (P, 7, D)),
        "qmask": qmask, "kmask": kmask, "ident": ident, "tri": tri, "nsel": nsel,
    }
    nc = _bacc.Bacc("TRN2", target_bir_lowering=False, num_devices=1)
    arrays, args = {}, []
    for name, v in laid.items():
        v = _np.ascontiguousarray(v)
        arrays[name] = v
        args.append(nc.dram_tensor(name, v.shape, _mybir.dt.from_np(v.dtype), kind="ExternalInput").ap())
    args.append(nc.dram_tensor("out", (B, T, D), F32, kind="ExternalOutput").ap())
    build(nc, *args)
    r = _run(nc, [arrays], core_ids=[0])
    return r.results[0]["out"]
```

```python
from collections import namedtuple
from contextlib import ExitStack

import numpy as np

import concourse.bass as bass
from concourse import mybir

F32 = mybir.dt.float32
F32R = mybir.dt.float32r
BF16 = mybir.dt.bfloat16
ALU = mybir.AluOpType
ACT = mybir.ActivationFunctionType
AX = mybir.AxisListType

P = 128
B, LX, FEATS = 64, 125, 32
STRIDE, PATCH = 8, 16
T = 1 + (LX - PATCH) // STRIDE
N = B * T
NT = N // P
D = 128
KP = PATCH * FEATS // P
JX = 2 * (T - 1) + KP
H, DH = 8, 16
R = H * T
EPS = 1e-5
NEG = -1e30
E, DHID = 10, 512
HC = DHID // P
KSH, KRC = 9, 3
HALVES = [(0, 512), (512, N)]
TILES = [range(0, 4), range(4, NT)]
TILE_RANGE = [slice(0, 4), slice(4, NT)]
G4 = 4
NG = B // G4
GV = 16

C_BQ, C_BK, C_BV, C_RC1 = range(4)
C_SH1 = 4
C_E1 = C_SH1 + HC
C_SH2 = C_E1 + E * HC
C_E2 = C_SH2 + 1
C_N = C_E2 + E
R_TOK, R_BO, R_GAMMA, R_BETA, R_RC2, R_LNG, R_LNB = range(7)
R_N = 7


NC1 = 2
FIRST_HALF = 1
LAST = (FIRST_HALF, 1 - FIRST_HALF)
NSHARED_FIRST = 5
KQ = 3 * DH
Job = namedtuple("Job", "expert half chunk width")
Unit = namedtuple("Unit", "expert half last")


def plan_jobs():
    def chunks(e, hf):
        return [Job(e, hf, c, HALVES[hf][1] - HALVES[hf][0]) for c in range(HC)]

    shared = chunks(None, 0) + chunks(None, 1)
    jobs, rest = shared[:NSHARED_FIRST], shared[NSHARED_FIRST:]
    for e in range(E):
        for hf in (FIRST_HALF, 1 - FIRST_HALF):
            jobs += chunks(e, hf)
            if rest and hf != FIRST_HALF:
                jobs.append(rest.pop(0))
    return jobs


JOBS = plan_jobs()
NJ = len(JOBS)
UNITS = [Unit(j.expert, j.half, n) for n, j in enumerate(JOBS) if j.chunk == HC - 1]
NUP, UP0 = 4, 2
NHID, NTT = 6, 3
NRAW, NWE, NGB = 4, 5, 4
LAG = 4
END_LAG = LAG + 1
LX_JOB, GT_STEP = 1, 2
NET = 4
QKV_BANK = [(4, 5), (6, 7), (0, 1)]
SPLITS = {0: (1,), 1: (2,), 2: (3,), 3: (4,)}


def last_job(e):
    return max(n for n, j in enumerate(JOBS) if j.expert == e)


def last_unit(e):
    return max(n for n, u in enumerate(UNITS) if u.expert == e)


for _e in range(NWE, E):
    SPLITS[last_job(_e - NWE) + LAG + 2] = (_e,)
GATES = {last_job(_e - NGB) + END_LAG + 2: (_e,) for _e in range(NGB, E)}


def dve_low(j):
    return j % 2 == 1


def lows(j, dve):
    return sum(dve_low(n) == dve for n in range(j + 1))


def unit_of(j):
    return next(n for n, u in enumerate(UNITS) if (u.expert, u.half) == (JOBS[j].expert, JOBS[j].half))


def parity(u):
    return sum(x.expert is not None for x in UNITS[:u]) % 2


def before(u):
    same = [n for n in range(u) if UNITS[n].expert is not None]
    return same[-2] if len(same) >= 2 else None


def ending(step):
    return [n for n, u in enumerate(UNITS) if u.last == step - END_LAG]


def conv_pieces(taps, half):
    lo, hi = HALVES[half]
    mid = taps // 2
    out = []
    for tap in [mid] + [k for k in range(taps) if k != mid]:
        d = (tap - mid) * B
        a, b = max(lo, -d), min(hi, N - d)
        if a < b:
            out.append((tap, a, b, a + d))
    return out


def build(nc, xT, wtok, wqkvo, wrc1, wrc2, wsh1, wsh2, we1, we2, cols, rows, qmask, kmask, ident, tri, out):
    with ExitStack() as ctx:
        def sb(name, shape, dt=F32, scope=ctx):
            return scope.enter_context(nc.sbuf_tensor(name, shape, dt))

        sems = {}

        def S(name):
            if name not in sems:
                sems[name] = ctx.enter_context(nc.semaphore(name))
            return sems[name]

        xT_s = sb("xT_s", [P, 2, JX // 2, B])
        wtok_s = sb("wtok_s", [P, KP, D])
        wqkvo_s = sb("wqkvo_s", [P, 4, D])
        wrc2_s = sb("wrc2_s", [P, KRC, E])
        wrc1_s = sb("wrc1_s", [P, KRC, D])
        wrc1_h = sb("wrc1_h", [P, KRC, D], F32R)
        wrc1_l = sb("wrc1_l", [P, KRC, D], F32R)
        raw = sb("raw", [P, KSH * DHID])
        wsh1_h = sb("wsh1_h", [P, KSH, DHID], F32R)
        wsh1_l = sb("wsh1_l", [P, KSH, DHID], F32R)
        wsh2_s = sb("wsh2_s", [P, HC, D])
        wsh2_h = sb("wsh2_h", [P, HC, D], F32R)
        wsh2_l = sb("wsh2_l", [P, HC, D], F32R)
        cols_s = sb("cols_s", [P, C_N])
        hcol = sb("hcol", [P, HC])
        rows_s = sb("rows_s", [P, R_N, D])
        ident_s = sb("ident_s", [P, P])
        tri_s = sb("tri_s", [P, E, E])
        rawr = raw[:].rearrange("p (s n) -> p s n", n=KSH * DHID // NRAW)[:, :, 0:2 * DHID]
        raw9 = raw[:].rearrange("p (k n) -> p k n", k=KSH)

        h = sb("h", [P, NT, D])
        x1 = sb("x1", [P, NT, D])
        x1bo = sb("x1bo", [P, NT, D])
        hbeta = sb("hbeta", [P, NT, D])
        xnT = sb("xnT", [P, N])
        cT = sb("cT", [P, N])
        xh = sb("xh", [P, N], F32R)
        xl = sb("xl", [P, N], F32R)
        o, on, rT, h2 = x1bo, x1, xnT, h
        zT = x1bo[:].rearrange("p i d -> p (i d)")
        yt = [t[:].rearrange("p i d -> p (i d)")[:, 0:512] for t in (x1, hbeta)]
        gatesT = cT[0:E, :]
        spare = xT_s[:].rearrange("p a j b -> p (a j b)")
        x3 = spare[:, 0:NT * D].rearrange("p (i d) -> p i d", d=D)
        z = spare[:, NT * D:2 * NT * D].rearrange("p (i d) -> p i d", d=D)
        stats = sb("stats", [P, 4, NT, 6])
        mv = sb("mv", [P, 4, NT, 2])
        veps = sb("veps", [P, 4, NT])
        rstd = sb("rstd", [P, 4, NT])
        mhalf = sb("mhalf", [P, NT])
        b2c = sb("b2c", [P, E])
        mx = sb("mx", [R, B])
        nmx = sb("nmx", [R, B], F32R)
        ones_f = sb("ones_f", [R, B])
        ones_r = sb("ones_r", [R, B], F32R)
        qm_f = sb("qm_f", [H, R])
        km_f = sb("km_f", [H, R])
        qm = sb("qm", [H, R], BF16)
        km = sb("km", [H, R], BF16)

        att = ExitStack()
        qk = sb("qk", [P, 4, N], F32R, att)
        vT = sb("vT", [P, N], F32, att)
        QR = sb("QR", [KQ + 1, R, B], F32R, att)
        KR = sb("KR", [KQ + 1, R, B], F32R, att)
        VR = sb("VR", [R, DH + 1, B], F32, att)
        ET = sb("ET", [R, NET, G4, R], F32, att)
        rden = sb("rden", [R, B], F32, att)
        CR = sb("CR", [R, DH, B], F32, att)
        att.close()
        WE_h = sb("WE_h", [P, NWE, 2 * DHID], F32R)
        WE_l = sb("WE_l", [P, NWE, 2 * DHID], F32R)
        Gb = sb("Gb", [P, NGB, N])
        rr = sb("rr", [P, 2, 512])
        ex = sb("ex", [P, 2, 512])
        tt = sb("tt", [P, NTT, 512])
        hh = sb("hh", [P, NHID, NC1 + 512], F32R)
        hl = sb("hl", [P, NHID, NC1 + 512], F32R)
        L = sb("L", [P, NT, E])
        m1 = sb("m1", [P, NT])
        Ld = sb("Ld", [P, NT, E])
        Lx = sb("Lx", [P, NT, E])
        gt, eq = (Gb[:, k, 0:NT * E * E].rearrange("p (i e f) -> p i e f", i=NT, e=E) for k in range(2))
        rank = sb("rank", [P, NT, E])
        gates = sb("gates", [P, NT, E])
        den = sb("den", [P, NT])

        v_dram = nc.dram_tensor("v_feat", (D, N), F32, kind="Internal").ap()
        c_dram = nc.dram_tensor("c_feat", (D, N), F32, kind="Internal").ap()
        qk_dram = nc.dram_tensor("qk_feat", (4, D, N), F32, kind="Internal").ap()
        g_dram = nc.dram_tensor("gates_feat", (E, N), F32, kind="Internal").ap()
        ps = [ctx.enter_context(nc.psum_tensor(f"bank{i}", [P, 512], F32)) for i in range(8)]

        block = ctx.enter_context(nc.Block())

        def tiles3(ap, n):
            return ap[:, 0:n * D].rearrange("p (i d) -> p i d", d=D)

        @block.sync
        def _(sp):
            for k in range(2):
                sp.dma_start(xT_s[:, k], xT[:, k]).then_inc(S("ld_x"), 16)
                if k == 0:
                    sp.dma_start(wtok_s[:], wtok).then_inc(S("ld_tok"), 16)
            for dst, src in ((rows_s, rows), (ident_s, ident), (cols_s, cols), (tri_s, tri), (qm_f, qmask), (km_f, kmask)):
                sp.dma_start(dst[:], src).then_inc(S("ld_cst"), 16)
            sp.dma_start(wqkvo_s[:], wqkvo).then_inc(S("ld_qkvo"), 16)
            for k in range(3):
                sp.dma_start(raw9[:, 3 * k:3 * k + 3, :], wsh1[:, 3 * k:3 * k + 3, :]).then_inc(S("ld_sh1"), 16)
            sp.dma_start(wsh2_s[:], wsh2).then_inc(S("ld_sh2"), 16)
            sp.dma_start(wrc1_s[:], wrc1).then_inc(S("ld_rc"), 16)
            sp.dma_start(wrc2_s[:], wrc2).then_inc(S("ld_rc"), 16)
            for n in range(4):
                sp.wait_ge(S("qkl_done" if n % 2 else "qkh_done"), 2 * (n // 2 + 1))
                sp.dma_start(qk_dram[n], qk[:, n, :].bitcast(F32)).then_inc(S("qk_out"), 16)
            sp.wait_ge(S("v_done"), 2)
            sp.dma_start(v_dram, vT[:]).then_inc(S("v_out"), 16)
            sp.wait_ge(S("qk_out"), 16 * 4)
            for dst, k, n in ((QR, 0, 0), (KR, 0, 2), (QR, 1, 0), (KR, 1, 3), (QR, 2, 1), (KR, 2, 2)):
                sp.dma_start(dst[k * DH:(k + 1) * DH].bitcast(F32).rearrange("e (c l) b -> e c (l b)", c=H),
                             qk_dram[n].rearrange("(c e) n -> e c n", e=DH)).then_inc(S("rows_in"), 16)
            sp.wait_ge(S("mask_done"), 3)
            sp.dma_start(KR[KQ:KQ + 1, :, :].bitcast(F32), ones_r[:].bitcast(F32)).then_inc(S("ones_in"), 16)
            sp.wait_ge(S("v_out"), 16)
            for c in range(H):
                sp.dma_start(VR[c * T:(c + 1) * T, 0:DH, :],
                             v_dram[c * DH:(c + 1) * DH, :].rearrange("e (l b) -> l e b", b=B)).then_inc(S("v_in"), 16)
            for k in range(2):
                sp.wait_ge(S("nmx_done"), k + 1)
                bs = slice(k * B // 2, (k + 1) * B // 2)
                sp.dma_start(QR[KQ:KQ + 1, :, bs].bitcast(F32), nmx[:, bs].bitcast(F32)).then_inc(S(f"mrow_in{k}"), 16)
            def load_expert(e):
                if e >= NRAW:
                    sp.wait_ge(S("we_l_done"), e - NRAW + 1)
                    sp.wait_ge(S("we_h_done"), e - NRAW + 1)
                sp.dma_start(rawr[:, e % NRAW, 0:DHID], we1[:, e, :]).then_inc(S(f"ld_e{e % NRAW}"), 16)
                sp.dma_start(rawr[:, e % NRAW, DHID:2 * DHID], we2[:, e].rearrange("p c d -> p (c d)")).then_inc(S(f"ld_e{e % NRAW}"), 16)

            sp.wait_ge(S("sh1_split"), 1)
            for e in range(NRAW):
                load_expert(e)
            for k in range(2):
                sp.wait_ge(S("ctx_done"), (k + 1) * B // GV // 2)
                bs = slice(k * B // 2, (k + 1) * B // 2)
                for c in range(H):
                    sp.dma_start(c_dram[c * DH:(c + 1) * DH, :].rearrange("e (l b) -> l e b", b=B)[:, :, bs],
                                 CR[c * T:(c + 1) * T, :, bs]).then_inc(S("c_out"), 16)
            sp.wait_ge(S("c_out"), 16 * 2 * H)
            sp.dma_start(cT[:], c_dram).then_inc(S("c_in"), 16)
            for e in range(NRAW, E):
                load_expert(e)
            for n, i in enumerate([i for hf in LAST for i in TILES[hf]]):
                sp.wait_ge(S("out_done"), n + 1)
                sp.dma_start(out[:, 2 * i:2 * i + 2, :].rearrange("b t d -> t b d"), z[:, i, :]).then_inc(S("stored"), 16)
            sp.wait_ge(S("stored"), 16 * NT)

        @block.gpsimd
        def _(pool):
            pool.memset(mhalf[:], -0.5).then_inc(S("pool_cst"), 1)
            pool.memset(VR[:, DH:DH + 1, :], 1.0).then_inc(S("pool_cst"), 1)
            pool.memset(ones_f[:], 1.0).then_inc(S("pool_cst"), 1)
            pool.wait_ge(S("pool_cst"), 3)

            def inv_std(n, k=0):
                pool.wait_ge(S("var_done"), n + k + 1)
                sl = TILE_RANGE[LAST[k]] if n == 3 else slice(0, NT)
                pool.tensor_tensor(rstd[:, n, sl], veps[:, n, sl], mhalf[:, sl], ALU.pow).then_inc(S("rstd_done"), 1)

            inv_std(0)
            pool.wait_ge(S("x1_done"), NT)
            pool.wait_ge(S("ld_cst"), 16 * 6)
            pool.tensor_tensor(x1bo[:], x1[:], rows_s[:, R_BO:R_BO + 1, :].broadcast_to([P, NT, D]), ALU.add).then_inc(S("x1bo_done"), 1)
            pool.tensor_tensor(hbeta[:], h[:], rows_s[:, R_BETA:R_BETA + 1, :].broadcast_to([P, NT, D]), ALU.add).then_inc(S("hbeta_done"), 1)
            for k in range(3):
                pool.wait_ge(S("w_h_done"), k + 1)
                ins = pool.tensor_tensor(wsh1_l[:, 3 * k:3 * k + 3, :], raw9[:, 3 * k:3 * k + 3, :], wsh1_h[:, 3 * k:3 * k + 3, :], ALU.subtract)
            ins.then_inc(S("sh1_split"), 1)
            pool.wait_ge(S("w_h_done"), 5)
            pool.tensor_tensor(wsh2_l[:], wsh2_s[:], wsh2_h[:], ALU.subtract).then_inc(S("sh2_split"), 1)
            pool.tensor_tensor(wrc1_l[:], wrc1_s[:], wrc1_h[:], ALU.subtract).then_inc(S("rc_split"), 1)
            for n in (1, 2):
                inv_std(n)

            def low(j):
                pool.wait_ge(S("hh_done"), j + 1)
                w = JOBS[j].width
                pool.tensor_tensor(hl[:, j % NHID, NC1:NC1 + w], tt[:, j % NTT, 0:w], hh[:, j % NHID, NC1:NC1 + w], ALU.subtract)\
                    .then_inc(S("hl_pool"), 1)

            pool.wait_ge(S("z_zero"), 1)

            def accumulate(u):
                lo, hi = HALVES[UNITS[u].half]
                pool.wait_ge(S("yt_done"), u + 1)
                if u:
                    pool.wait_ge(S("z_add"), u)
                pool.tensor_tensor(zT[:, lo:hi], zT[:, lo:hi], yt[u % 2][:, 0:hi - lo], ALU.add).then_inc(S("z_add"), 1)

            for step in range(NJ + END_LAG):
                if step < NJ and not dve_low(step):
                    low(step)
                for u in ending(step):
                    accumulate(u)
            for k in range(2):
                inv_std(3, k)

        @block.tensor
        def _(pe):
            mm = nc.tensor.matmul
            pe.wait_ge(S("ld_x"), 32)
            pe.wait_ge(S("ld_tok"), 16)
            for hf in range(2):
                for i in TILES[hf]:
                    col = (i - TILES[hf][0]) * D
                    for k in range(KP):
                        a = 2 * i + k // 2
                        ins = mm(ps[hf][:, col:col + D], xT_s[:, k % 2, a:a + 2, :], wtok_s[:, k, :],
                                 start=(k == 0), stop=(k == KP - 1))
                ins.then_inc(S("tok_mm"), 1)

            def transposes(src, done, banks, tag):
                for hf in range(2):
                    pe.wait_ge(S(done), TILES[hf][-1] + 1)
                    for i in TILES[hf]:
                        col = (i - TILES[hf][0]) * P
                        ins = nc.tensor.transpose(ps[banks[hf]][:, col:col + P], src[:, i, :], ident_s[:])
                    ins.then_inc(S(tag), 1)

            pe.wait_ge(S("ld_cst"), 16 * 6)
            transposes(x1, "x1_done", (2, 3), "x1T_mm")
            pe.wait_ge(S("ld_qkvo"), 16)
            for n in range(3):
                for hf, (lo, hi) in enumerate(HALVES):
                    pe.wait_ge(S("x1T_done"), hf + 1)
                    mm(ps[QKV_BANK[n][hf]][:, 0:hi - lo], wqkvo_s[:, n, :], xnT[:, lo:hi], start=True, stop=True).then_inc(S("qkv_mm"), 1)

            def group(bank, st, sm, g):
                mm(ps[bank][0:R, 0:G4 * R], qm[:], km[:].rearrange("p (o r) -> p o r", o=1).broadcast_to([H, G4, R]),
                   start=True, stop=False)
                for j in range(G4):
                    b = g * G4 + j
                    q_ap, k_ap = QR[0:KQ + sm, :, b], KR[0:KQ + sm, :, b]
                    ins = mm(ps[bank][0:R, j * R:(j + 1) * R], k_ap if sm else q_ap, q_ap if sm else k_ap,
                             start=False, stop=(j == G4 - 1))
                ins.then_inc(S(st), 1)

            pe.wait_ge(S("rows_in"), 16 * 6)
            pe.wait_ge(S("mask_done"), 3)
            pe.wait_ge(S("v_done"), 2)
            for g in range(NG):
                if g >= 4:
                    pe.wait_ge(S("mx_done"), g - 3)
                group(g % 4, "s_mm", False, g)

            def context(g):
                pe.wait_ge(S("exp_done"), g + 1)
                for j in range(G4):
                    b = g * G4 + j
                    col = (b % GV) * (DH + 1)
                    ins = mm(ps[4 + b // GV][0:R, col:col + DH + 1], ET[:, g % NET, j, :], VR[:, :, b], start=True, stop=True)
                ins.then_inc(S("ctx_mm"), 1)

            pe.wait_ge(S("v_in"), 16 * H)
            pe.wait_ge(S("ones_in"), 16)
            pe.wait_ge(S("mx_done"), NG)
            for g in range(NG):
                pe.wait_ge(S(f"mrow_in{g * 2 // NG}"), 16)
                if g >= 4:
                    pe.wait_ge(S("exp_done"), g - 3)
                group(g % 4, "st_mm", True, g)
                if g:
                    context(g - 1)
            context(NG - 1)
            pe.wait_ge(S("c_in"), 16)
            for hf in range(2):
                for i in TILES[hf]:
                    col = (i - TILES[hf][0]) * D
                    ins = mm(ps[hf][:, col:col + D], cT[:, i * P:(i + 1) * P], wqkvo_s[:, 3, :], start=True, stop=True)
                ins.then_inc(S("o_mm"), 1)
            transposes(x3, "x3_done", (2, 3), "x3T_mm")

            def three(o_ap, w_h, w_l, x_h, x_l, first, last):
                mm(o_ap, w_h, x_h, start=first, stop=False)
                mm(o_ap, w_h, x_l, start=False, stop=False)
                return mm(o_ap, w_l, x_h, start=False, stop=last)

            def conv(bank, hf, w_h, w_l, taps):
                lo, _ = HALVES[hf]
                pieces = conv_pieces(taps, hf)
                for n, (tap, a, b, src) in enumerate(pieces):
                    ins = three(ps[bank][:, a - lo:b - lo], w_h(tap), w_l(tap), xh[:, src:src + b - a], xl[:, src:src + b - a],
                                n == 0, n == len(pieces) - 1)
                return ins

            def up(j):
                job = JOBS[j]
                lo, hi = HALVES[job.half]
                if j >= NUP:
                    pe.wait_ge(S("a2_done"), j - NUP + 1)
                bank = UP0 + j % NUP
                c = job.chunk
                if job.expert is None:
                    ins = conv(bank, job.half, lambda k: wsh1_h[:, k, c * P:(c + 1) * P],
                               lambda k: wsh1_l[:, k, c * P:(c + 1) * P], KSH)
                else:
                    e = job.expert
                    pe.wait_ge(S("we_l_done"), e + 1)
                    ins = three(ps[bank][:, 0:hi - lo], WE_h[:, e % NWE, c * P:(c + 1) * P], WE_l[:, e % NWE, c * P:(c + 1) * P],
                                xh[:, lo:hi], xl[:, lo:hi], True, True)
                ins.then_inc(S("up_mm"), 1)

            def down(j):
                job = JOBS[j]
                w = job.width
                c = job.chunk
                if dve_low(j):
                    pe.wait_ge(S("hl_dve"), lows(j, True))
                else:
                    pe.wait_ge(S("hl_pool"), lows(j, False))
                if job.expert is None:
                    bank, (w_h, w_l) = job.half, (wsh2_h[:, c, :], wsh2_l[:, c, :])
                else:
                    u = unit_of(j)
                    bank = 6 + parity(u)
                    if c == 0:
                        prev = before(u)
                        if prev is not None:
                            pe.wait_ge(S("yt_done"), prev + 1)
                        else:
                            pe.wait_ge(S("gT_done"), 2)
                    sl = slice(DHID + c * P, DHID + (c + 1) * P)
                    w_h, w_l = WE_h[:, job.expert % NWE, sl], WE_l[:, job.expert % NWE, sl]
                a = 0 if job.expert is not None and NC1 + w <= 512 else NC1
                three(ps[bank][:, 0:NC1 + w - a], w_h, w_l, hh[:, j % NHID, a:NC1 + w], hl[:, j % NHID, a:NC1 + w],
                      c == 0, c == HC - 1).then_inc(S("down_mm"), 1)

            pe.wait_ge(S("ld_rc"), 32)
            pe.wait_ge(S("rc_split"), 1)
            for hf in range(2):
                if hf == 0:
                    pe.wait_ge(S("xl_done"), 2)
                conv(6 + hf, hf, lambda k: wrc1_h[:, k, :], lambda k: wrc1_l[:, k, :], KRC).then_inc(S("rc1_mm"), 1)
            pe.wait_ge(S("sh1_split"), 1)
            pe.wait_ge(S("sh2_split"), 1)
            pe.wait_ge(S("z_zero"), 3)
            for step in range(NJ + LAG):
                if step < NJ:
                    up(step)
                if step == 0:
                    pe.wait_ge(S("gelu_done"), 2)
                    for i in range(NT):
                        o_ap = ps[7][:, i * E:(i + 1) * E]
                        a = i * P
                        mm(o_ap, rT[:, a:a + P], wrc2_s[:, 1, :], start=(i == 0), stop=False)
                        for tap, d in ((2, B), (0, -B)):
                            whole = 0 <= a + d and a + d + P <= N
                            if whole:
                                ins = mm(o_ap, rT[:, a + d:a + d + P], wrc2_s[:, tap, :], start=False, stop=(i == NT - 1))
                            elif d < 0:
                                ins = mm(ps[7][B:P, i * E:(i + 1) * E], rT[:, 0:B], wrc2_s[:, tap, :], start=False, stop=False)
                            else:
                                ins = mm(ps[7][0:B, i * E:(i + 1) * E], rT[:, N - B:N], wrc2_s[:, tap, :], start=False, stop=False)
                    ins.then_inc(S("L_mm"), 1)
                if step == GT_STEP:
                    pe.wait_ge(S("gates_done"), 1)
                    for hf in range(2):
                        for i in TILES[hf]:
                            col = (i - TILES[hf][0]) * P
                            ins = nc.tensor.transpose(ps[6 + hf][0:E, col:col + P], gates[:, i, :], ident_s[:])
                        ins.then_inc(S("gT_mm"), 1)
                if step >= LAG:
                    down(step - LAG)
            for n, hf in enumerate(LAST):
                pe.wait_ge(S("z_add"), len(UNITS) - 1 + n)
                lo, _ = HALVES[hf]
                for i in TILES[hf]:
                    j = i - TILES[hf][0]
                    ins = nc.tensor.transpose(ps[2 + hf][:, j * P:(j + 1) * P], zT[:, lo + j * P:lo + (j + 1) * P], ident_s[:])
                ins.then_inc(S("z_mm"), 1)

        @block.scalar
        def _(act):
            A = nc.scalar.activation
            act.wait_ge(S("ld_cst"), 16 * 6)
            act.wait_ge(S("pool_cst"), 3)
            A(qm[:], qm_f[:], ACT.Copy).then_inc(S("mask_done"), 1)
            A(km[:], km_f[:], ACT.Copy).then_inc(S("mask_done"), 1)
            A(ones_r[:], ones_f[:], ACT.Copy).then_inc(S("mask_done"), 1)
            A(hcol[:], cols_s[:, C_SH1:C_SH1 + HC], ACT.Copy, scale=0.5).then_inc(S("hcol_done"), 1)
            for hf, (lo, hi) in enumerate(HALVES):
                act.wait_ge(S("x1T_mm"), hf + 1)
                A(xnT[:, lo:hi], ps[2 + hf][:, 0:hi - lo], ACT.Copy).then_inc(S("x1T_done"), 1)
            for n in range(2):
                for hf, (lo, hi) in enumerate(HALVES):
                    act.wait_ge(S("qkv_mm"), 2 * n + hf + 1)
                    A(qk[:, 2 * n, lo:hi], ps[QKV_BANK[n][hf]][:, 0:hi - lo], ACT.Identity,
                      bias=cols_s[:, C_BQ + n:C_BQ + n + 1]).then_inc(S("qkh_done"), 1)
            for hf, (lo, hi) in enumerate(HALVES):
                act.wait_ge(S("qkv_mm"), 4 + hf + 1)
                A(vT[:, lo:hi], ps[QKV_BANK[2][hf]][:, 0:hi - lo], ACT.Identity,
                  bias=cols_s[:, C_BV:C_BV + 1]).then_inc(S("v_done"), 1)
            for k in range(3):
                act.wait_ge(S("ld_sh1"), 16 * 3)
                A(wsh1_h[:, 3 * k:3 * k + 3, :], raw9[:, 3 * k:3 * k + 3, :], ACT.Copy).then_inc(S("w_h_done"), 1)
            act.wait_ge(S("ld_sh2"), 16)
            A(wsh2_h[:], wsh2_s[:], ACT.Copy).then_inc(S("w_h_done"), 1)
            act.wait_ge(S("ld_rc"), 32)
            A(wrc1_h[:], wrc1_s[:], ACT.Copy).then_inc(S("w_h_done"), 1)
            for g in range(NG):
                act.wait_ge(S("st_mm"), g + 1)
                if g >= NET:
                    act.wait_ge(S("ctx_mm"), g - NET + 1)
                A(ET[:, g % NET], ps[g % 4][0:R, 0:G4 * R].rearrange("p (j r) -> p j r", j=G4), ACT.Exp,
                  scale=float(DH) ** -0.5).then_inc(S("exp_done"), 1)

            def split_high(e):
                act.wait_ge(S(f"ld_e{e % NRAW}"), 32 * (e // NRAW + 1))
                if e >= NWE:
                    act.wait_ge(S("down_mm"), last_job(e - NWE) + 1)
                A(WE_h[:, e % NWE, :], rawr[:, e % NRAW, :], ACT.Copy).then_inc(S("we_h_done"), 1)

            act.wait_ge(S("c_in"), 16)
            for hf, (lo, hi) in enumerate(HALVES):
                if hf == 0:
                    split_high(0)
                act.wait_ge(S("x3T_mm"), hf + 1)
                A(xh[:, lo:hi], ps[2 + hf][:, 0:hi - lo], ACT.Copy).then_inc(S("xh_done"), 1)
            for hf, (lo, hi) in enumerate(HALVES):
                act.wait_ge(S("rc1_mm"), hf + 1)
                A(rT[:, lo:hi], ps[6 + hf][:, 0:hi - lo], ACT.Gelu, bias=cols_s[:, C_RC1:C_RC1 + 1]).then_inc(S("gelu_done"), 1)

            for j, job in enumerate(JOBS):
                w = job.width
                shared = job.expert is None
                bias = hcol[:, job.chunk:job.chunk + 1] if shared else \
                    cols_s[:, C_E1 + job.expert * HC + job.chunk:C_E1 + job.expert * HC + job.chunk + 1]
                act.wait_ge(S("up_mm"), j + 1)
                if j >= 2:
                    act.wait_ge(S("tt_done"), j - 1)
                A(rr[:, j % 2, 0:w], ps[UP0 + j % NUP][:, 0:w], ACT.Identity if shared else ACT.Relu, bias=bias,
                  scale=0.5 if shared else 1.0).then_inc(S("a1_done"), 1)
                A(ex[:, j % 2, 0:w], ps[UP0 + j % NUP][:, 0:w], ACT.Tanh if shared else ACT.Exp, bias=bias,
                  scale=0.5 if shared else 1.0).then_inc(S("a2_done"), 1)
                if j == LX_JOB:
                    act.wait_ge(S("Ld_done"), 1)
                    A(Lx[:], Ld[:], ACT.Exp).then_inc(S("Lx_done"), 1)
                if j == GT_STEP + 1:
                    act.wait_ge(S("gT_done"), 2)
                    act.dma_start(g_dram, gatesT).then_inc(S("g_out"), 16)
                if j == GT_STEP + 2:
                    act.wait_ge(S("g_out"), 16)
                    for e in range(NGB):
                        act.dma_start(Gb[:, e, :], g_dram[e:e + 1, :].broadcast_to([P, N])).then_inc(S(f"Gb_in{e}"), 16)
                for e in SPLITS.get(j, ()):
                    split_high(e)
                for e in GATES.get(j, ()):
                    act.wait_ge(S("yt_done"), last_unit(e - NGB) + 1)
                    act.dma_start(Gb[:, e % NGB, :], g_dram[e:e + 1, :].broadcast_to([P, N])).then_inc(S(f"Gb_in{e % NGB}"), 16)

        @block.vector
        def _(dve):
            V = nc.vector
            chain = [0]

            def link(ins):
                chain[0] += 1
                ins.then_inc(S("dve_chain"), 1)
                dve.wait_ge(S("dve_chain"), chain[0])

            def bc(row):
                return rows_s[:, row:row + 1, :]

            def layernorm_stats(n, src, tiles=range(NT), k=0):
                for i in tiles:
                    ins = V.bn_stats(stats[:, n, i, :], src[:, i, :])
                link(ins)
                for i in tiles:
                    ins = V.bn_aggr(mv[:, n, i, :], stats[:, n, i, :])
                link(ins)
                sl = slice(tiles[0], tiles[-1] + 1)
                V.tensor_scalar(veps[:, n, sl], mv[:, n, sl, 1], EPS, None, ALU.add).then_inc(S("var_done"), 1)
                dve.wait_ge(S("rstd_done"), n + k + 1)

            def normalise(n, dst, src, tag, tiles=range(NT)):
                for i in tiles:
                    V.tensor_scalar(dst[:, i, :], src[:, i, :], mv[:, n, i, 0:1], rstd[:, n, i:i + 1],
                                    ALU.subtract, ALU.mult).then_inc(S(tag), 1)

            dve.wait_ge(S("ld_cst"), 16 * 6)
            for hf in range(2):
                dve.wait_ge(S("tok_mm"), hf + 1)
                n = len(TILES[hf])
                i0 = TILES[hf][0]
                link(V.tensor_tensor(h[:, i0:i0 + n, :], tiles3(ps[hf], n), bc(R_TOK).broadcast_to([P, n, D]), ALU.add))
            layernorm_stats(0, h)
            normalise(0, x1, h, "x1_done")
            for n in range(2):
                for hf, (lo, hi) in enumerate(HALVES):
                    dve.wait_ge(S("qkh_done"), 2 * n + hf + 1)
                    V.scalar_tensor_tensor(qk[:, 2 * n + 1, lo:hi], ps[QKV_BANK[n][hf]][:, 0:hi - lo],
                                           cols_s[:, C_BQ + n:C_BQ + n + 1], qk[:, 2 * n, lo:hi], ALU.add, ALU.subtract)\
                        .then_inc(S("qkl_done"), 1)
            for g in range(NG):
                dve.wait_ge(S("s_mm"), g + 1)
                V.tensor_reduce(mx[:, g * G4:(g + 1) * G4], ps[g % 4][0:R, 0:G4 * R].rearrange("p (j s) -> p j s", j=G4),
                                AX.X, ALU.max).then_inc(S("mx_done"), 1)
                if (g + 1) % (NG // 2) == 0:
                    k = g // (NG // 2)
                    bs = slice(k * B // 2, (k + 1) * B // 2)
                    dve.wait_ge(S("mx_done"), g + 1)
                    V.tensor_scalar(nmx[:, bs], mx[:, bs], -1.0, None, ALU.mult).then_inc(S("nmx_done"), 1)
            for g in range(B // GV):
                dve.wait_ge(S("ctx_mm"), (g + 1) * GV // G4)
                acc = ps[4 + g][0:R, 0:GV * (DH + 1)].rearrange("p (b e) -> p b e", e=DH + 1)
                rd = rden[:, g * GV:(g + 1) * GV]
                link(V.reciprocal(rd, acc[:, :, DH]))
                V.tensor_tensor(CR[:, :, g * GV:(g + 1) * GV].rearrange("p e b -> p b e"), acc[:, :, 0:DH],
                                rd.rearrange("p (b o) -> p b o", o=1).broadcast_to([R, GV, DH]),
                                ALU.mult).then_inc(S("ctx_done"), 1)
            for hf in range(2):
                dve.wait_ge(S("o_mm"), hf + 1)
                dve.wait_ge(S("x1bo_done"), 1)
                n = len(TILES[hf])
                i0 = TILES[hf][0]
                link(V.tensor_tensor(o[:, i0:i0 + n, :], tiles3(ps[hf], n), x1bo[:, i0:i0 + n, :], ALU.add))
            layernorm_stats(1, o)
            normalise(1, on, o, "on_done")
            dve.wait_ge(S("on_done"), NT)
            dve.wait_ge(S("hbeta_done"), 1)
            link(V.tensor_tensor(on[:], on[:], bc(R_GAMMA).broadcast_to([P, NT, D]), ALU.mult))
            link(V.tensor_tensor(h2[:], on[:], hbeta[:], ALU.add))
            layernorm_stats(2, h2)
            normalise(2, x3, h2, "x3_done")
            for hf, (lo, hi) in enumerate(HALVES):
                dve.wait_ge(S("xh_done"), hf + 1)
                V.tensor_tensor(xl[:, lo:hi], ps[2 + hf][:, 0:hi - lo], xh[:, lo:hi], ALU.subtract).then_inc(S("xl_done"), 1)

            def split_low(e):
                dve.wait_ge(S("we_h_done"), e + 1)
                V.tensor_tensor(WE_l[:, e % NWE, :], rawr[:, e % NRAW, :], WE_h[:, e % NWE, :], ALU.subtract)\
                    .then_inc(S("we_l_done"), 1)

            def router_a():
                dve.wait_ge(S("L_mm"), 1)
                link(V.tensor_tensor(L[:], ps[7][:, 0:NT * E].rearrange("p (i e) -> p i e", e=E),
                                     rows_s[:, R_RC2:R_RC2 + 1, 0:E].broadcast_to([P, NT, E]), ALU.add))
                link(V.tensor_reduce(m1[:], L[:], AX.X, ALU.max))
                V.tensor_tensor(Ld[:], L[:], m1[:].rearrange("p (i o) -> p i o", o=1).broadcast_to([P, NT, E]),
                                ALU.subtract).then_inc(S("Ld_done"), 1)

            def router_b():
                other = L[:].rearrange("p i (o f) -> p i o f", o=1).broadcast_to([P, NT, E, E])
                mine = L[:].rearrange("p i (e o) -> p i e o", o=1).broadcast_to([P, NT, E, E])
                V.tensor_tensor(gt, other, mine, ALU.is_gt)
                link(V.tensor_tensor(eq, other, mine, ALU.is_equal))
                link(V.tensor_tensor(eq, eq, tri_s[:].rearrange("p (o e) f -> p o e f", o=1).broadcast_to([P, NT, E, E]),
                                     ALU.mult))
                link(V.tensor_tensor(gt, gt, eq, ALU.add))
                link(V.tensor_reduce(rank[:], gt, AX.X, ALU.add))
                dve.wait_ge(S("Lx_done"), 1)
                link(V.scalar_tensor_tensor(gates[:], rank[:], 1.5, Lx[:], ALU.is_lt, ALU.mult))
                link(V.tensor_reduce(den[:], gates[:], AX.X, ALU.add))
                link(V.reciprocal(den[:], den[:]))
                V.tensor_tensor(gates[:], gates[:], den[:].rearrange("p (i o) -> p i o", o=1).broadcast_to([P, NT, E]),
                                ALU.mult).then_inc(S("gates_done"), 1)

            def job_body(j):
                job = JOBS[j]
                w = job.width
                dve.wait_ge(S("a2_done"), j + 1)
                if j >= NTT:
                    dve.wait_ge(S("hl_pool"), lows(j - NTT, False))
                    dve.wait_ge(S("hl_dve"), lows(j - NTT, True)) if lows(j - NTT, True) else None
                shared = job.expert is None
                V.scalar_tensor_tensor(tt[:, j % NTT, 0:w], ex[:, j % 2, 0:w], 1.0, rr[:, j % 2, 0:w],
                                       ALU.add if shared else ALU.min, ALU.mult if shared else ALU.add)\
                    .then_inc(S("tt_done"), 1)
                dve.wait_ge(S("tt_done"), j + 1)
                if j >= NHID:
                    dve.wait_ge(S("down_mm"), j - NHID + 1)
                V.tensor_copy(hh[:, j % NHID, NC1:NC1 + w], tt[:, j % NTT, 0:w]).then_inc(S("hh_done"), 1)
                if dve_low(j):
                    dve.wait_ge(S("hh_done"), j + 1)
                    V.tensor_tensor(hl[:, j % NHID, NC1:NC1 + w], tt[:, j % NTT, 0:w], hh[:, j % NHID, NC1:NC1 + w], ALU.subtract)\
                        .then_inc(S("hl_dve"), 1)

            def unit_end(u):
                unit = UNITS[u]
                lo, hi = HALVES[unit.half]
                dve.wait_ge(S("down_mm"), unit.last + 1)
                if u >= 2:
                    dve.wait_ge(S("z_add"), u - 1)
                if unit.expert is None:
                    V.tensor_scalar(yt[u % 2][:, 0:hi - lo], ps[unit.half][:, 0:hi - lo], cols_s[:, C_SH2:C_SH2 + 1],
                                    None, ALU.add).then_inc(S("yt_done"), 1)
                else:
                    dve.wait_ge(S(f"Gb_in{unit.expert % NGB}"), 16 * (unit.expert // NGB + 1))
                    bank, e = ps[6 + parity(u)], unit.expert
                    a = NC1 if unit.half == FIRST_HALF else 0
                    if a:
                        link(V.tensor_tensor(b2c[:, e:e + 1], bank[:, 0:1], cols_s[:, C_E2 + e:C_E2 + e + 1], ALU.add))
                    V.scalar_tensor_tensor(yt[u % 2][:, 0:hi - lo], bank[:, a:a + hi - lo], b2c[:, e:e + 1],
                                           Gb[:, e % NGB, lo:hi], ALU.add, ALU.mult).then_inc(S("yt_done"), 1)

            split_low(0)
            V.memset(zT, 0.0).then_inc(S("z_zero"), 1)
            V.memset(hh[:, :, 0:NC1].bitcast(F32), -1.0).then_inc(S("z_zero"), 1)
            V.memset(hl[:, :, 0:NC1].bitcast(F32), 0.0).then_inc(S("z_zero"), 1)
            for step in range(NJ + END_LAG):
                if step < NJ:
                    job_body(step)
                if step == LX_JOB - 1:
                    router_a()
                if step == LX_JOB:
                    router_b()
                if step == LX_JOB:
                    pass
                if step == GT_STEP:
                    for hf, (lo, hi) in enumerate(HALVES):
                        dve.wait_ge(S("gT_mm"), hf + 1)
                        V.tensor_copy(gatesT[:, lo:hi], ps[6 + hf][0:E, 0:hi - lo]).then_inc(S("gT_done"), 1)
                for e in SPLITS.get(step, ()):
                    split_low(e)
                for u in ending(step):
                    unit_end(u)
            link(V.tensor_tensor(h2[:], h2[:], bc(R_LNB).broadcast_to([P, NT, D]), ALU.add))
            for k, hf in enumerate(LAST):
                dve.wait_ge(S("z_mm"), k + 1)
                n = len(TILES[hf])
                i0 = TILES[hf][0]
                link(V.tensor_tensor(z[:, i0:i0 + n, :], tiles3(ps[2 + hf], n), x3[:, i0:i0 + n, :], ALU.add))
                layernorm_stats(3, z, TILES[hf], k)
                normalise(3, z, z, "zn_done", TILES[hf])
                dve.wait_ge(S("zn_done"), n if k == 0 else NT)
                link(V.tensor_tensor(z[:, i0:i0 + n, :], z[:, i0:i0 + n, :], bc(R_LNG).broadcast_to([P, n, D]), ALU.mult))
                for i in TILES[hf]:
                    V.tensor_tensor(z[:, i, :], z[:, i, :], h2[:, i, :], ALU.add).then_inc(S("out_done"), 1)


def shape_constants():
    c, l = np.divmod(np.arange(R), T)
    head = (l * H + c) // T
    same = (np.arange(H)[:, None] == head[None, :]).astype(np.float32)
    q, k = same, np.where(same > 0, 0.0, NEG).astype(np.float32)
    tri = np.ascontiguousarray(np.broadcast_to(np.tril(np.ones((E, E), np.float32), -1), (P, E, E)))
    return q, k, np.eye(P, dtype=np.float32), tri


def kernel(**inputs):
    import numpy as _np
    import concourse.bacc as _bacc
    from concourse import mybir as _mybir
    from concourse.bass_utils import run_bass_kernel_spmd as _run

    a = {k: _np.asarray(v) for k, v in inputs.items()}
    f = lambda n: a["L0_ffn_" + n]
    at = lambda n: a["L0_attn_" + n]
    colv = _np.zeros((P, C_N), _np.float32)
    for n, name in ((C_BQ, "bq"), (C_BK, "bk"), (C_BV, "bv")):
        colv[:, n] = at(name)
    colv[:, C_RC1] = f("rc_b1")
    colv[:, C_SH2] = f("sh_b2")
    colv[:, C_E2:] = f("e_b2").T
    colv[:, C_SH1:C_E1] = f("sh_b1").reshape(HC, P).T
    colv[:, C_E1:C_SH2] = f("e_b1").reshape(E * HC, P).T
    rc2 = _np.zeros(D, _np.float32)
    rc2[:E] = f("rc_b2")
    rowv = _np.stack([a["L0_tok_b"], at("bo"), at("gamma"), at("beta"), rc2, f("ln_g"), f("ln_b")])
    qmask, kmask, ident, tri = shape_constants()
    laid = {
        "xT": a["x"].reshape(B, LX * FEATS)[:, :JX * P].reshape(B, JX // 2, 2, P).transpose(3, 2, 1, 0),
        "wtok": a["L0_tok_W"].T.reshape(KP, P, D).transpose(1, 0, 2),
        "wqkvo": _np.stack([at("Wq").T, at("Wk").T, at("Wv").T, at("Wo").T], axis=1),
        "wrc1": f("rc_w1").transpose(1, 2, 0),
        "wrc2": f("rc_w2").transpose(1, 2, 0),
        "wsh1": f("sh_w1").transpose(1, 2, 0),
        "wsh2": f("sh_w2")[:, :, 0].T.reshape(HC, P, D).transpose(1, 0, 2),
        "we1": f("e_w1").transpose(1, 0, 2),
        "we2": f("e_w2").reshape(E, HC, P, D).transpose(2, 0, 1, 3),
        "cols": colv,
        "rows": _np.broadcast_to(rowv[None], (P, R_N, D)),
        "qmask": qmask, "kmask": kmask, "ident": ident, "tri": tri,
    }
    nc = _bacc.Bacc("TRN2", target_bir_lowering=False, num_devices=1)
    arrays, args = {}, []
    for name, v in laid.items():
        v = _np.ascontiguousarray(v)
        arrays[name] = v
        args.append(nc.dram_tensor(name, v.shape, _mybir.dt.from_np(v.dtype), kind="ExternalInput").ap())
    args.append(nc.dram_tensor("out", (B, T, D), F32, kind="ExternalOutput").ap())
    build(nc, *args)
    r = _run(nc, [arrays], core_ids=[0])
    return r.results[0]["out"]
```

```python
from collections import namedtuple
from contextlib import ExitStack

import numpy as np

import concourse.bass as bass
from concourse import mybir

F32 = mybir.dt.float32
F32R = mybir.dt.float32r
ALU = mybir.AluOpType
ACT = mybir.ActivationFunctionType
AX = mybir.AxisListType

P = 128
B, LX, FEATS = 64, 125, 32
STRIDE, PATCH = 8, 16
T = 1 + (LX - PATCH) // STRIDE
N = B * T
NT = N // P
D = 128
KP = PATCH * FEATS // P
JX = 2 * (T - 1) + KP
H, DH = 8, 16
R = H * T
EPS = 1e-5
NEG = -1e30
E, DHID = 10, 512
HC = DHID // P
KSH, KRC = 9, 3
HALVES = [(0, 512), (512, N)]
X_PARTS = [1, 3, NT]
TILES = [range(0, 4), range(4, NT)]
TILE_RANGE = [slice(0, 4), slice(4, NT)]
G4 = 4
NG = B // G4

QUAD = 32

C_BQ, C_BK, C_BV, C_RC1 = range(4)
C_SH1 = 4
C_E1 = C_SH1 + HC
C_SH2 = C_E1 + E * HC
C_E2 = C_SH2 + 1
C_N = C_E2 + E
R_TOK, R_BO, R_GAMMA, R_BETA, R_RC2, R_LNG, R_LNB = range(7)
R_N = 7

NET = 4
CTX_PARTS = [(0, 32), (32, 48), (48, B)]
QKV_BANK = [(4, 5), (6, 7), (0, 1)]
KQ = H + 3 * DH
VCOLS = 32 + DH
ACT_TILES = 2
HW = N // 2
FHALVES = [(0, HW), (HW, N)]
END_TILES = [range(0, HW // P), range(HW // P, NT)]
NC1 = 2
Job = namedtuple("Job", "expert chunk")
JOBS = [Job(e, c) for e in [None] + list(range(E)) for c in range(HC)]
NJ = len(JOBS)
NU = E + 1
OUT0 = 4
NHID, NTT = 5, 3
NRAW, NWE, NGB = 4, 3, 3
LAG = 4
END_LAG = LAG
LX_JOB, GT_STEP = 1, 3


def last_job(e):
    return HC * (e + 2) - 1


SPLITS = {1: [(1, 0), (1, 1)], 2: [(2, 0), (2, 1)]}
for _e in range(NWE, E):
    SPLITS[last_job(_e - NWE) + LAG + 1] = [(_e, 0)]
    SPLITS[last_job(_e - NWE) + LAG + 3] = [(_e, 1)]


def dve_low(j):
    return j % 2 == 1


def lows(j, dve):
    return sum(dve_low(n) == dve for n in range(j + 1))


def ending(step):
    u, c = divmod(step - END_LAG, HC)
    return u if u >= 0 and c == HC - 1 else None


def conv_pieces(taps, half):
    lo, hi = FHALVES[half]
    mid = taps // 2
    out = []
    for tap in [mid] + [k for k in range(taps) if k != mid]:
        d = (tap - mid) * B
        a, b = max(lo, -d), min(hi, N - d)
        if a < b:
            out.append((tap, a, b, a + d))
    return out


def build(nc, xT, wtok, wqkvo, wrc1, wrc2, wsh1, wsh2, we1, we2, cols, rows, qmask, kmask, ident, tri, taps, out):
    with ExitStack() as ctx:
        def sb(name, shape, dt=F32, scope=ctx):
            return scope.enter_context(nc.sbuf_tensor(name, shape, dt))

        sems = {}

        def S(name):
            if name not in sems:
                sems[name] = ctx.enter_context(nc.semaphore(name))
            return sems[name]

        xT_s = sb("xT_s", [P, 2, JX // 2, B])
        wtok_s = sb("wtok_s", [P, KP, D])
        wqkvo_s = sb("wqkvo_s", [P, 4, D])
        wrc2_s = sb("wrc2_s", [P, KRC, QUAD])
        wrc1_s = sb("wrc1_s", [P, KRC, D])
        wrc1_h = sb("wrc1_h", [P, KRC, D], F32R)
        wrc1_l = sb("wrc1_l", [P, KRC, D], F32R)
        raw = sb("raw", [P, KSH * DHID])
        wsh1_h = sb("wsh1_h", [P, KSH, DHID], F32R)
        wsh1_l = sb("wsh1_l", [P, KSH, DHID], F32R)
        wsh2_s = sb("wsh2_s", [P, HC, D])
        wsh2_h = sb("wsh2_h", [P, HC, D], F32R)
        wsh2_l = sb("wsh2_l", [P, HC, D], F32R)
        cols_s = sb("cols_s", [P, C_N])
        hcol = sb("hcol", [P, HC])
        rows_s = sb("rows_s", [P, R_N, D])
        ident_s = sb("ident_s", [P, P])
        taps_s = sb("taps_s", [KRC * QUAD, E])
        tri_s = sb("tri_s", [P, E, E])
        rawr = raw[:].rearrange("p (s n) -> p s n", n=KSH * DHID // NRAW)[:, :, 0:2 * DHID]
        raw9 = raw[:].rearrange("p (k n) -> p k n", k=KSH)

        h = sb("h", [P, NT, D])
        x1 = sb("x1", [P, NT, D])
        x1bo = sb("x1bo", [P, NT, D])
        hbeta = sb("hbeta", [P, NT, D])
        xnT = sb("xnT", [P, N])
        cT = sb("cT", [P, T, B])
        xh = sb("xh", [P, N], F32R)
        xl = sb("xl", [P, N], F32R)
        gatesT = cT[0:E].rearrange("e l b -> e (l b)")
        on, rT, h2 = x1, xnT, h
        zT = x1bo[:].rearrange("p i d -> p (i d)")
        yt = [t[:].rearrange("p i d -> p (i d)") for t in (x1, hbeta)]
        spare = xT_s[:].rearrange("p a j b -> p (a j b)")
        cx = spare[:, 0:2 * N].rearrange("p (l k b) -> p l k b", k=2, b=B)
        x3 = spare[:, 0:NT * D].rearrange("p (i d) -> p i d", d=D)
        z = spare[:, NT * D:2 * NT * D].rearrange("p (i d) -> p i d", d=D)
        stats = sb("stats", [P, 4, NT, 6])
        mv = sb("mv", [P, 4, NT, 2])
        veps = sb("veps", [P, 4, NT])
        rstd = sb("rstd", [P, 4, NT])
        nmr = sb("nmr", [P, 4, NT])
        mhalf = sb("mhalf", [P, NT])
        b2c = sb("b2c", [P, E])
        mx = sb("mx", [R, B])
        nmx = sb("nmx", [R, B], F32R)
        ones_f = sb("ones_f", [R, B])
        ones_r = sb("ones_r", [R, B], F32R)
        qm_f = sb("qm_f", [H, R])
        km_f = sb("km_f", [H, R])

        att = ExitStack()
        QR = sb("QR", [KQ + 1, R, B], F32R, att)
        KR = sb("KR", [KQ + 1, R, B], F32R, att)
        qk = sb("qk", [P, 4, N], F32R, att)
        vT = sb("vT", [P, N], F32, att)
        VR = sb("VR", [P, VCOLS, B], F32, att)
        ET = qk[:].bitcast(F32).rearrange("p n (j r) -> p n j r", r=R)[:, :, 0:G4]
        att.close()
        ctx_rows = ExitStack()
        CR = sb("CR", [DH, R * 2, B], F32, ctx_rows)
        ctx_rows.close()
        CR4 = CR[:].rearrange("e (r k) b -> e r k b", k=2)
        WE_h = sb("WE_h", [P, NWE, 2 * DHID], F32R)
        WE_l = sb("WE_l", [P, NWE, 2 * DHID], F32R)
        Gb = sb("Gb", [P, NGB, N])
        rr = sb("rr", [P, 2, N])
        ex = sb("ex", [P, 2, N])
        tt = sb("tt", [P, NTT, N])
        hh = sb("hh", [P, NHID, 2, NC1 + HW], F32R)
        hl = sb("hl", [P, NHID, 2, NC1 + HW], F32R)
        L = sb("L", [P, NT, E])
        m1 = sb("m1", [P, NT])
        Ld = sb("Ld", [P, NT, E])
        Lx = sb("Lx", [P, NT, E])
        gt, eq = (Gb[:, k, 0:NT * E * E].rearrange("p (i e f) -> p i e f", i=NT, e=E) for k in range(2))
        Lf = Gb[0:KRC * QUAD, 2, :]
        rank = sb("rank", [P, NT, E])
        gates = L
        den = sb("den", [P, NT])

        v_dram = nc.dram_tensor("v_feat", (D, N), F32, kind="Internal").ap()
        qk_dram = nc.dram_tensor("qk_feat", (4, D, N), F32, kind="Internal").ap()
        g_dram = nc.dram_tensor("gates_feat", (E, N), F32, kind="Internal").ap()
        psum = ctx.enter_context(nc.psum_tensor("psum", [P, 8, 512], F32))
        ps = [psum[:, i, :] for i in range(8)]

        block = ctx.enter_context(nc.Block())

        def halves(ap):
            return ap.rearrange("p (h n) -> p h n", h=2)

        def pre_activations(j):
            return psum[:, 2 * (j % 2):2 * (j % 2) + 2, 0:HW]

        def tiles3(ap, n):
            return ap[:, 0:n * D].rearrange("p (i d) -> p i d", d=D)

        def tile_list(t):
            return [t[:, i, :] for i in range(NT)]

        def bank_tiles(banks, groups):
            return [ps[b][:, (i - g[0]) * D:(i - g[0] + 1) * D] for b, g in zip(banks, groups) for i in g]

        h_t, x1_t, x3_t, on_t, h2_t, z_t = (tile_list(t) for t in (h, x1, x3, on, h2, z))
        o_ps = bank_tiles((0, 1), TILES)
        z_ps = bank_tiles((0, 1), END_TILES)

        def ln_tiles(n, k):
            return (END_TILES if n == 3 else TILES)[k]

        def tile_range(n, k):
            return slice(ln_tiles(n, k)[0], ln_tiles(n, k)[-1] + 1)

        def gather_chunk(queue, k, c):
            bs = slice(*CTX_PARTS[k])
            queue.dma_start(spare[c * DH:(c + 1) * DH, 0:2 * N].rearrange("p (n b) -> p n b", b=B)[:, :, bs],
                            CR[:, 2 * c * T:2 * (c + 1) * T, bs]).then_inc(S(f"c_in{k}"), 16)

        @block.sync
        def _(sp):
            for dst, src in ((qm_f, qmask), (km_f, kmask)):
                sp.dma_start(dst[:], src).then_inc(S("ld_mask"), 16)
            for k, tiles in enumerate(X_PARTS):
                a = 2 * X_PARTS[k - 1] + 1 if k else 0
                b = 2 * tiles + 1
                sp.dma_start(xT_s[:, :, a:b], xT[:, :, a:b]).then_inc(S(f"ld_x{k}"), 16)
                if k == 0:
                    sp.dma_start(wtok_s[:], wtok).then_inc(S("ld_tok"), 16)
            for dst, src in ((rows_s, rows), (ident_s, ident), (cols_s, cols), (tri_s, tri), (taps_s, taps)):
                sp.dma_start(dst[:], src).then_inc(S("ld_cst"), 16)
            sp.dma_start(wqkvo_s[:], wqkvo).then_inc(S("ld_qkvo"), 16)
            for k in range(3):
                sp.dma_start(raw9[:, 3 * k:3 * k + 3, :], wsh1[:, 3 * k:3 * k + 3, :]).then_inc(S("ld_sh1"), 16)
            sp.dma_start(wsh2_s[:], wsh2).then_inc(S("ld_sh2"), 16)
            sp.dma_start(wrc1_s[:], wrc1).then_inc(S("ld_rc"), 16)
            sp.dma_start(wrc2_s[:], wrc2).then_inc(S("ld_rc"), 16)
            for low in range(2):
                for hf, (lo, hi) in enumerate(HALVES):
                    for m in range(2):
                        n = 2 * m + low
                        sp.wait_ge(S("qkl_done" if low else "qkh_done"), 2 * hf + m + 1)
                        sp.dma_start(qk_dram[n][:, lo:hi], qk[:, n, lo:hi].bitcast(F32)).then_inc(S(f"qk_out{n}"), 16)
            for dst, k, n in ((QR, 0, 0), (QR, 1, 0), (KR, 0, 2), (KR, 2, 2), (QR, 2, 1), (KR, 1, 3)):
                sp.wait_ge(S(f"qk_out{n}"), 32)
                a = H + k * DH
                sp.dma_start(dst[a:a + DH].bitcast(F32).rearrange("e (c l) b -> e c (l b)", c=H),
                             qk_dram[n].rearrange("(c e) n -> e c n", e=DH)).then_inc(S("rows_in"), 16)
            sp.wait_ge(S("v_done"), 2)
            sp.dma_start(v_dram, vT[:]).then_inc(S("v_out"), 16)
            sp.wait_ge(S("ones_done"), 1)
            sp.dma_start(KR[KQ:KQ + 1, :, :].bitcast(F32), ones_r[:].bitcast(F32)).then_inc(S("ones_in"), 16)
            sp.wait_ge(S("v_out"), 16)
            sp.wait_ge(S("pool_cst"), 3)
            for c in range(H):
                sp.dma_start(VR[c * T:(c + 1) * T, 0:DH, :],
                             v_dram[c * DH:(c + 1) * DH, :].rearrange("e (l b) -> l e b", b=B)).then_inc(S("v_in"), 16)
            for k in range(2):
                sp.wait_ge(S("nmx_done"), k + 1)
                bs = slice(k * B // 2, (k + 1) * B // 2)
                sp.dma_start(QR[KQ:KQ + 1, :, bs].bitcast(F32), nmx[:, bs].bitcast(F32)).then_inc(S(f"mrow_in{k}"), 16)

            def load_expert(e):
                if e >= NRAW:
                    sp.wait_ge(S("we_l_done"), 2 * (e - NRAW + 1))
                    sp.wait_ge(S("we_h_done"), 2 * (e - NRAW + 1))
                sp.dma_start(rawr[:, e % NRAW, 0:DHID], we1[:, e, :]).then_inc(S(f"ld_e{e % NRAW}"), 16)
                sp.dma_start(rawr[:, e % NRAW, DHID:2 * DHID], we2[:, e].rearrange("p c d -> p (c d)")).then_inc(S(f"ld_e{e % NRAW}"), 16)

            sp.wait_ge(S("sh1_split"), 1)
            for e in range(NRAW):
                load_expert(e)
            for k, (_, b1) in enumerate(CTX_PARTS):
                sp.wait_ge(S("num_done"), b1 // G4)
                sp.wait_ge(S("den_done"), b1 // G4)
                for c in range(0, H, 2 if k == len(CTX_PARTS) - 1 else 1):
                    gather_chunk(sp, k, c)

            def load_gates(e):
                if e >= NGB:
                    sp.wait_ge(S("yt_done"), e - NGB + 2)
                sp.dma_start(Gb[:, e % NGB, :], g_dram[e:e + 1, :].broadcast_to([P, N])).then_inc(S(f"Gb_in{e % NGB}"), 16)

            loaded = NRAW
            sp.wait_ge(S("g_out"), 16)
            for e in range(E):
                load_gates(e)
                if loaded < E:
                    load_expert(loaded)
                    loaded += 1
            for i in range(NT):
                sp.wait_ge(S("out_done"), i + 1)
                sp.dma_start(out[:, 2 * i:2 * i + 2, :].rearrange("b t d -> t b d"), z[:, i, :]).then_inc(S("stored"), 16)
            sp.wait_ge(S("stored"), 16 * NT)

        @block.gpsimd
        def _(pool):
            pool.memset(mhalf[:], -0.5).then_inc(S("pool_cst"), 1)
            pool.memset(VR[:], 1.0).then_inc(S("pool_cst"), 1)
            pool.memset(ones_f[:], 1.0).then_inc(S("pool_cst"), 1)
            pool.wait_ge(S("pool_cst"), 3)

            def inv_std(n, k):
                pool.wait_ge(S("var_done"), 2 * n + k + 1)
                sl = tile_range(n, k)
                pool.tensor_tensor(rstd[:, n, sl], veps[:, n, sl], mhalf[:, sl], ALU.pow).then_inc(S("rstd_done"), 1)

            for k in range(2):
                inv_std(0, k)
            pool.wait_ge(S("x1_act"), 2 * ACT_TILES)
            pool.wait_ge(S("x1_dve"), NT - 2 * ACT_TILES)
            pool.wait_ge(S("ld_cst"), 16 * 5)
            pool.tensor_tensor(x1bo[:], x1[:], rows_s[:, R_BO:R_BO + 1, :].broadcast_to([P, NT, D]), ALU.add).then_inc(S("x1bo_done"), 1)
            pool.tensor_tensor(hbeta[:], h[:], rows_s[:, R_BETA:R_BETA + 1, :].broadcast_to([P, NT, D]), ALU.add).then_inc(S("hbeta_done"), 1)
            for k in range(3):
                pool.wait_ge(S("w_h_done"), k + 1)
                ins = pool.tensor_tensor(wsh1_l[:, 3 * k:3 * k + 3, :], raw9[:, 3 * k:3 * k + 3, :], wsh1_h[:, 3 * k:3 * k + 3, :], ALU.subtract)
            ins.then_inc(S("sh1_split"), 1)
            pool.wait_ge(S("w_h_done"), 5)
            pool.tensor_tensor(wsh2_l[:], wsh2_s[:], wsh2_h[:], ALU.subtract).then_inc(S("sh2_split"), 1)
            pool.tensor_tensor(wrc1_l[:], wrc1_s[:], wrc1_h[:], ALU.subtract).then_inc(S("rc_split"), 1)
            for n in (1, 2):
                for k in range(2):
                    inv_std(n, k)

            def low(j, part, tag):
                pool.wait_ge(S("hh_done"), j + 1)
                pool.tensor_tensor(hl[:, j % NHID, part, NC1:], halves(tt[:, j % NTT, :])[:, part, :],
                                   hh[:, j % NHID, part, NC1:], ALU.subtract).then_inc(S(tag), 1)

            def split_low(e, m):
                pool.wait_ge(S("we_h_done"), 2 * e + m + 1)
                sl = slice(m * DHID, (m + 1) * DHID)
                pool.tensor_tensor(WE_l[:, e % NWE, sl], rawr[:, e % NRAW, sl], WE_h[:, e % NWE, sl], ALU.subtract)\
                    .then_inc(S("we_l_done"), 1)

            def accumulate(u):
                pool.wait_ge(S("yt_done"), u + 1)
                if u:
                    pool.wait_ge(S("z_add"), u)
                pool.tensor_tensor(zT, zT, yt[u % 2], ALU.add).then_inc(S("z_add"), 1)

            for m in range(2):
                split_low(0, m)
            pool.wait_ge(S("z_zero"), 1)
            for step in range(NJ + END_LAG):
                if step < NJ and not dve_low(step):
                    low(step, slice(0, 2), "hl_pool")
                for e, m in SPLITS.get(step + 1, ()):
                    split_low(e, m)
                u = ending(step)
                if u is not None and u < NU - 2:
                    accumulate(u)
                if step == NJ - 1:
                    low(NJ - 1, slice(1, 2), "hl_last")
            for k in range(2):
                inv_std(3, k)

        @block.tensor
        def _(pe):
            mm = nc.tensor.matmul
            pe.wait_ge(S("ld_tok"), 16)
            for hf in range(2):
                for i in TILES[hf]:
                    for k, tiles in enumerate(X_PARTS):
                        if i == (X_PARTS[k - 1] if k else 0):
                            pe.wait_ge(S(f"ld_x{k}"), 16)
                    col = (i - TILES[hf][0]) * D
                    for k in range(KP):
                        a = 2 * i + k // 2
                        ins = mm(ps[hf][:, col:col + D], xT_s[:, k % 2, a:a + 2, :], wtok_s[:, k, :],
                                 start=(k == 0), stop=(k == KP - 1))
                ins.then_inc(S("tok_mm"), 1)

            def transposes(src, done, banks, tag):
                for hf in range(2):
                    pe.wait_ge(S(done + "_act"), ACT_TILES * (hf + 1))
                    pe.wait_ge(S(done + "_dve"), TILES[hf][-1] + 1 - ACT_TILES * (hf + 1))
                    for i in TILES[hf]:
                        col = (i - TILES[hf][0]) * P
                        ins = nc.tensor.transpose(ps[banks[hf]][:, col:col + P], src[:, i, :], ident_s[:])
                    ins.then_inc(S(tag), 1)

            pe.wait_ge(S("ld_cst"), 16 * 5)
            transposes(x1, "x1", (2, 3), "x1T_mm")
            pe.wait_ge(S("ld_qkvo"), 16)
            for n, hf in [(0, 0), (1, 0), (0, 1), (1, 1), (2, 0), (2, 1)]:
                lo, hi = HALVES[hf]
                pe.wait_ge(S("x1T_done"), hf + 1)
                mm(ps[QKV_BANK[n][hf]][:, 0:hi - lo], wqkvo_s[:, n, :], xnT[:, lo:hi], start=True, stop=True).then_inc(S("qkv_mm"), 1)

            def group(bank, st, sm, g):
                for j in range(G4):
                    b = g * G4 + j
                    q_ap, k_ap = QR[0:KQ + sm, :, b], KR[0:KQ + sm, :, b]
                    ins = mm(ps[bank][0:R, j * R:(j + 1) * R], k_ap if sm else q_ap, q_ap if sm else k_ap,
                             start=True, stop=True)
                ins.then_inc(S(st), 1)

            pe.wait_ge(S("rows_in"), 16 * 6)
            pe.wait_ge(S("mask_done"), 2)
            pe.wait_ge(S("v_done"), 2)
            for g in range(NG):
                if g >= 4:
                    pe.wait_ge(S("mx_done"), g - 3)
                group(g % 4, "s_mm", False, g)

            def context(g):
                pe.wait_ge(S("exp_done"), g + 1)
                if g >= 4:
                    pe.wait_ge(S("num_done"), g - 3)
                    pe.wait_ge(S("den_done"), g - 3)
                for j in range(G4):
                    ins = mm(ps[4 + g % 4][0:VCOLS, j * R:(j + 1) * R], VR[:, :, g * G4 + j], ET[:, g % NET, j, :],
                             start=True, stop=True)
                ins.then_inc(S("ctx_mm"), 1)

            def residual(bank, src, tiles):
                mm(ps[bank][:, 0:len(tiles) * D], ident_s[:], src[:, tiles[0]:tiles[-1] + 1, :], start=True, stop=False)

            pe.wait_ge(S("v_in"), 16 * H)
            pe.wait_ge(S("ones_in"), 16)
            pe.wait_ge(S("mx_done"), NG)
            for g in range(NG):
                pe.wait_ge(S(f"mrow_in{g * 2 // NG}"), 16)
                if g >= 4:
                    pe.wait_ge(S("exp_done"), g - 3)
                group(g % 4, "st_mm", True, g)
                if g:
                    context(g - 1)
            context(NG - 1)
            pe.wait_ge(S("x1bo_done"), 1)
            for hf in range(2):
                residual(hf, x1bo, TILES[hf])
            for hf in range(2):
                pe.wait_ge(S("c_done"), hf + 1)
                for i in TILES[hf]:
                    ins = mm(o_ps[i], cT[:, 2 * i:2 * i + 2, :].rearrange("p l b -> p (l b)"), wqkvo_s[:, 3, :],
                             start=False, stop=(i == TILES[hf][-1]))
                ins.then_inc(S("o_mm"), 1)
            transposes(x3, "x3", (2, 3), "x3T_mm")

            def three(o_ap, w_h, w_l, x_h, x_l, first, last):
                mm(o_ap, w_h, x_h, start=first, stop=False)
                mm(o_ap, w_h, x_l, start=False, stop=False)
                return mm(o_ap, w_l, x_h, start=False, stop=last)

            def conv(bank, hf, w_h, w_l, taps):
                lo, _ = FHALVES[hf]
                pieces = conv_pieces(taps, hf)
                for n, (tap, a, b, src) in enumerate(pieces):
                    ins = three(ps[bank][:, a - lo:b - lo], w_h(tap), w_l(tap), xh[:, src:src + b - a], xl[:, src:src + b - a],
                                n == 0, n == len(pieces) - 1)
                return ins

            def up(j):
                e, c = JOBS[j]
                if j >= 2:
                    pe.wait_ge(S("a2_done"), j - 1)
                if e is not None and c == 0:
                    pe.wait_ge(S("we_l_done"), 2 * e + 1)
                cs = slice(c * P, (c + 1) * P)
                for hf, (lo, hi) in enumerate(FHALVES):
                    bank = 2 * (j % 2) + hf
                    if e is None:
                        ins = conv(bank, hf, lambda k: wsh1_h[:, k, cs], lambda k: wsh1_l[:, k, cs], KSH)
                    else:
                        ins = three(ps[bank][:, 0:HW], WE_h[:, e % NWE, cs], WE_l[:, e % NWE, cs],
                                    xh[:, lo:hi], xl[:, lo:hi], True, True)
                ins.then_inc(S("up_mm"), 1)

            def down(j):
                u, c = divmod(j, HC)
                e = JOBS[j].expert
                if dve_low(j):
                    pe.wait_ge(S("hl_dve"), lows(j, True))
                else:
                    pe.wait_ge(S("hl_pool"), lows(j, False))
                if c == 0 and u == 1:
                    pe.wait_ge(S("gT_done"), 2)
                if c == 0 and u >= 2:
                    pe.wait_ge(S("yt_done"), u - 1)
                if e is not None and c == 0:
                    pe.wait_ge(S("we_l_done"), 2 * e + 2)
                if e is None:
                    a, w_h, w_l = NC1, wsh2_h[:, c, :], wsh2_l[:, c, :]
                else:
                    sl = slice(DHID + c * P, DHID + (c + 1) * P)
                    a, w_h, w_l = 0, WE_h[:, e % NWE, sl], WE_l[:, e % NWE, sl]
                for hf in range(2):
                    if j == NJ - 1 and hf == 1:
                        pe.wait_ge(S("hl_last"), 1)
                    ins = three(ps[OUT0 + 2 * (u % 2) + hf][:, 0:NC1 + HW - a], w_h, w_l,
                                hh[:, j % NHID, hf, a:], hl[:, j % NHID, hf, a:], c == 0, c == HC - 1)
                ins.then_inc(S("down_mm"), 1)

            def add_back(src, k, last=False):
                for i in END_TILES[k]:
                    ins = mm(z_ps[i], src[:, i * P:(i + 1) * P], ident_s[:], start=False, stop=(last and i == END_TILES[k][-1]))
                return ins

            pe.wait_ge(S("ld_rc"), 32)
            pe.wait_ge(S("rc_split"), 1)
            for hf in range(2):
                pe.wait_ge(S("xl_done"), hf + 1)
                conv(6 + hf, hf, lambda k: wrc1_h[:, k, :], lambda k: wrc1_l[:, k, :], KRC).then_inc(S("rc1_mm"), 1)
            pe.wait_ge(S("sh1_split"), 1)
            pe.wait_ge(S("sh2_split"), 1)
            pe.wait_ge(S("z_zero"), 3)
            for step in range(NJ + LAG):
                if step < NJ:
                    up(step)
                if step == 0:
                    pe.wait_ge(S("gelu_done"), 2)
                    for hf, (lo, hi) in enumerate(FHALVES):
                        ins = mm(ps[6 + hf][0:KRC * QUAD, 0:HW], wrc2_s[:].rearrange("p k e -> p (k e)"), rT[:, lo:hi],
                                 start=True, stop=True)
                    ins.then_inc(S("taps_mm"), 1)
                if step == 1:
                    pe.wait_ge(S("taps_done"), 2 * KRC)
                    for i in range(NT):
                        ins = mm(ps[7][:, i * E:(i + 1) * E], Lf[:, i * P:(i + 1) * P], taps_s[:], start=True, stop=True)
                    ins.then_inc(S("L_mm"), 1)
                if step == GT_STEP:
                    pe.wait_ge(S("gates_done"), 1)
                    for hf in range(2):
                        for i in TILES[hf]:
                            col = (i - TILES[hf][0]) * P
                            ins = nc.tensor.transpose(ps[6 + hf][0:E, col:col + P], gates[:, i, :], ident_s[:])
                        ins.then_inc(S("gT_mm"), 1)
                if step >= LAG:
                    down(step - LAG)
                if step == NJ - 1:
                    pe.wait_ge(S("a2_done"), NJ - 1)
                    for k in range(2):
                        residual(k, x3, END_TILES[k])
                    pe.wait_ge(S("z_add"), NU - 2)
                    for k in range(2):
                        add_back(zT, k)
            pe.wait_ge(S("yt_done"), NU - 1)
            for k in range(2):
                add_back(yt[(NU - 2) % 2], k)
            for k in range(2):
                pe.wait_ge(S("yt_done"), NU + k)
                add_back(yt[(NU - 1) % 2], k, True).then_inc(S("z_mm"), 1)

        @block.scalar
        def _(act):
            A = nc.scalar.activation
            act.wait_ge(S("ld_mask"), 32)
            A(KR[0:H], km_f[:].rearrange("h (r o) -> h r o", o=1).broadcast_to([H, R, B]), ACT.Copy).then_inc(S("mask_done"), 1)
            act.wait_ge(S("pool_cst"), 3)
            A(ones_r[:], ones_f[:], ACT.Copy).then_inc(S("ones_done"), 1)
            act.wait_ge(S("ld_cst"), 16 * 5)
            A(hcol[:], cols_s[:, C_SH1:C_SH1 + HC], ACT.Copy, scale=0.5).then_inc(S("hcol_done"), 1)

            def normalise(n, dst, src, hf, tag):
                act.wait_ge(S("nmr_done"), 2 * n + hf + 1)
                for i in TILES[hf][:None if n == 1 else ACT_TILES]:
                    A(dst[i], src[i], ACT.Identity, bias=nmr[:, n, i:i + 1], scale=rstd[:, n, i:i + 1]).then_inc(S(tag), 1)

            for hf in range(2):
                normalise(0, x1_t, h_t, hf, "x1_act")
            for hf, (lo, hi) in enumerate(HALVES):
                act.wait_ge(S("x1T_mm"), hf + 1)
                A(xnT[:, lo:hi], ps[2 + hf][:, 0:hi - lo], ACT.Copy).then_inc(S("x1T_done"), 1)
            for hf, (lo, hi) in enumerate(HALVES):
                for n in range(2):
                    act.wait_ge(S("qkv_mm"), 2 * hf + n + 1)
                    A(qk[:, 2 * n, lo:hi], ps[QKV_BANK[n][hf]][:, 0:hi - lo], ACT.Identity,
                      bias=cols_s[:, C_BQ + n:C_BQ + n + 1]).then_inc(S("qkh_done"), 1)
            for hf, (lo, hi) in enumerate(HALVES):
                act.wait_ge(S("qkv_mm"), 4 + hf + 1)
                A(vT[:, lo:hi], ps[QKV_BANK[2][hf]][:, 0:hi - lo], ACT.Identity,
                  bias=cols_s[:, C_BV:C_BV + 1]).then_inc(S("v_done"), 1)
            for k in range(3):
                act.wait_ge(S("ld_sh1"), 16 * 3)
                A(wsh1_h[:, 3 * k:3 * k + 3, :], raw9[:, 3 * k:3 * k + 3, :], ACT.Copy).then_inc(S("w_h_done"), 1)
            act.wait_ge(S("ld_sh2"), 16)
            A(wsh2_h[:], wsh2_s[:], ACT.Copy).then_inc(S("w_h_done"), 1)
            act.wait_ge(S("ld_rc"), 32)
            A(wrc1_h[:], wrc1_s[:], ACT.Copy).then_inc(S("w_h_done"), 1)

            def denominators(g):
                act.wait_ge(S("ctx_mm"), g + 1)
                A(CR4[:, :, 1, g * G4:(g + 1) * G4].rearrange("e r b -> e b r"),
                  ps[4 + g % 4][32:VCOLS, 0:G4 * R].rearrange("e (b r) -> e b r", b=G4), ACT.Copy).then_inc(S("den_done"), 1)

            act.wait_ge(S("ET_zero"), 1)
            for g in range(NG):
                act.wait_ge(S("st_mm"), g + 1)
                if g >= NET:
                    act.wait_ge(S("ctx_mm"), g - NET + 1)
                A(ET[0:R, g % NET], ps[g % 4][0:R, 0:G4 * R].rearrange("p (j r) -> p j r", j=G4), ACT.Exp,
                  scale=float(DH) ** -0.5).then_inc(S("exp_done"), 1)
                if g:
                    denominators(g - 1)
            denominators(NG - 1)

            def split_high(e, m):
                act.wait_ge(S(f"ld_e{e % NRAW}"), 32 * (e // NRAW + 1))
                if e >= NWE:
                    act.wait_ge(S("down_mm"), last_job(e - NWE) + 1)
                sl = slice(m * DHID, (m + 1) * DHID)
                A(WE_h[:, e % NWE, sl], rawr[:, e % NRAW, sl], ACT.Copy).then_inc(S("we_h_done"), 1)

            act.wait_ge(S("num_done"), NG)
            act.wait_ge(S("den_done"), NG)
            for c in range(1, H, 2):
                gather_chunk(act, len(CTX_PARTS) - 1, c)
            act.wait_ge(S("c_done"), 2)
            for m in range(2):
                split_high(0, m)
            for hf in range(2):
                normalise(1, on_t, o_ps, hf, "on_done")
            for hf in range(2):
                normalise(2, x3_t, h2_t, hf, "x3_act")
            for hf, (lo, hi) in enumerate(HALVES):
                act.wait_ge(S("x3T_mm"), hf + 1)
                A(xh[:, lo:hi], ps[2 + hf][:, 0:hi - lo], ACT.Copy).then_inc(S("xh_done"), 1)
            for hf, (lo, hi) in enumerate(FHALVES):
                act.wait_ge(S("rc1_mm"), hf + 1)
                A(rT[:, lo:hi], ps[6 + hf][:, 0:HW], ACT.Gelu, bias=cols_s[:, C_RC1:C_RC1 + 1]).then_inc(S("gelu_done"), 1)

            for j, (e, c) in enumerate(JOBS):
                shared = e is None
                bias = hcol[:, c:c + 1] if shared else cols_s[:, C_E1 + e * HC + c:C_E1 + e * HC + c + 1]
                act.wait_ge(S("up_mm"), j + 1)
                if j >= 2:
                    act.wait_ge(S("tt_done"), j - 1)
                A(halves(rr[:, j % 2, :]), pre_activations(j), ACT.Identity if shared else ACT.Relu, bias=bias,
                  scale=0.5 if shared else 1.0).then_inc(S("a1_done"), 1)
                A(halves(ex[:, j % 2, :]), pre_activations(j), ACT.Tanh if shared else ACT.Exp, bias=bias,
                  scale=0.5 if shared else 1.0).then_inc(S("a2_done"), 1)
                if j == LX_JOB:
                    act.wait_ge(S("Ld_done"), 1)
                    A(Lx[:], Ld[:], ACT.Exp).then_inc(S("Lx_done"), 1)
                if j == GT_STEP + 1:
                    act.wait_ge(S("gT_done"), 2)
                    act.dma_start(g_dram, gatesT).then_inc(S("g_out"), 16)
                for e, m in SPLITS.get(j, ()):
                    split_high(e, m)

        @block.vector
        def _(dve):
            V = nc.vector
            chain = [0]

            def link(ins):
                chain[0] += 1
                ins.then_inc(S("dve_chain"), 1)
                dve.wait_ge(S("dve_chain"), chain[0])

            def bc(row):
                return rows_s[:, row:row + 1, :]

            def ln_stats(n, src, hf):
                for i in ln_tiles(n, hf):
                    ins = V.bn_stats(stats[:, n, i, :], src[i])
                link(ins)
                for i in ln_tiles(n, hf):
                    ins = V.bn_aggr(mv[:, n, i, :], stats[:, n, i, :])
                link(ins)
                sl = tile_range(n, hf)
                V.tensor_scalar(veps[:, n, sl], mv[:, n, sl, 1], EPS, None, ALU.add).then_inc(S("var_done"), 1)

            def ln_bias(n, hf):
                dve.wait_ge(S("rstd_done"), 2 * n + hf + 1)
                sl = TILE_RANGE[hf]
                V.scalar_tensor_tensor(nmr[:, n, sl], mv[:, n, sl, 0], -1.0, rstd[:, n, sl], ALU.mult, ALU.mult)\
                    .then_inc(S("nmr_done"), 1)

            def normalise(n, dst, src, hf, tag):
                for i in ln_tiles(n, hf)[ACT_TILES:]:
                    V.tensor_scalar(dst[i], src[i], mv[:, n, i, 0:1], rstd[:, n, i:i + 1], ALU.subtract, ALU.mult)\
                        .then_inc(S(tag), 1)

            def ln_affine(n, dst, tmp, src, gain, shift, hf, tag):
                for i in ln_tiles(n, hf):
                    ins = V.scalar_tensor_tensor(tmp[i], src[i], mv[:, n, i, 0:1], rows_s[:, gain, :],
                                                 ALU.subtract, ALU.mult)
                link(ins)
                for i in ln_tiles(n, hf):
                    V.scalar_tensor_tensor(dst[i], tmp[i], rstd[:, n, i:i + 1], shift[i],
                                           ALU.mult, ALU.add).then_inc(S(tag), 1)

            dve.wait_ge(S("ld_mask"), 32)
            V.tensor_copy(QR[0:H], qm_f[:].rearrange("h (r o) -> h r o", o=1).broadcast_to([H, R, B])).then_inc(S("mask_done"), 1)
            dve.wait_ge(S("ld_cst"), 16 * 5)
            for hf in range(2):
                dve.wait_ge(S("tok_mm"), hf + 1)
                n = len(TILES[hf])
                i0 = TILES[hf][0]
                link(V.tensor_tensor(h[:, i0:i0 + n, :], tiles3(ps[hf], n), bc(R_TOK).broadcast_to([P, n, D]), ALU.add))
                ln_stats(0, h_t, hf)
            for hf in range(2):
                ln_bias(0, hf)
                normalise(0, x1_t, h_t, hf, "x1_dve")
            for hf, (lo, hi) in enumerate(HALVES):
                for n in range(2):
                    dve.wait_ge(S("qkh_done"), 2 * hf + n + 1)
                    V.scalar_tensor_tensor(qk[:, 2 * n + 1, lo:hi], ps[QKV_BANK[n][hf]][:, 0:hi - lo],
                                           cols_s[:, C_BQ + n:C_BQ + n + 1], qk[:, 2 * n, lo:hi], ALU.add, ALU.subtract)\
                        .then_inc(S("qkl_done"), 1)
            for n in range(4):
                dve.wait_ge(S(f"qk_out{n}"), 32)
            V.memset(ET[96:P], 0.0).then_inc(S("ET_zero"), 1)
            for g in range(NG):
                dve.wait_ge(S("s_mm"), g + 1)
                V.tensor_reduce(mx[:, g * G4:(g + 1) * G4], ps[g % 4][0:R, 0:G4 * R].rearrange("p (j s) -> p j s", j=G4),
                                AX.X, ALU.max).then_inc(S("mx_done"), 1)
                if (g + 1) % (NG // 2) == 0:
                    k = g // (NG // 2)
                    bs = slice(k * B // 2, (k + 1) * B // 2)
                    dve.wait_ge(S("mx_done"), g + 1)
                    V.tensor_scalar(nmx[:, bs], mx[:, bs], -1.0, None, ALU.mult).then_inc(S("nmx_done"), 1)
            def invert(k, hf):
                sl = TILE_RANGE[hf]
                den = cx[:, 2 * sl.start:2 * sl.stop, 1, slice(*CTX_PARTS[k])]
                return V.reciprocal(den, den)

            for g in range(NG):
                dve.wait_ge(S("ctx_mm"), g + 1)
                V.tensor_copy(CR4[:, :, 0, g * G4:(g + 1) * G4].rearrange("e r b -> e b r"),
                              ps[4 + g % 4][0:DH, 0:G4 * R].rearrange("e (b r) -> e b r", b=G4)).then_inc(S("num_done"), 1)
                if g == NG - 3:
                    dve.wait_ge(S("c_in0"), 16 * H)
                    invert(0, 0)
                if g == NG - 2:
                    invert(0, 1)
            for k in range(1, len(CTX_PARTS)):
                dve.wait_ge(S(f"c_in{k}"), 16 * H)
                if k < len(CTX_PARTS) - 1:
                    for hf in range(2):
                        invert(k, hf)
            for hf in range(2):
                link(invert(len(CTX_PARTS) - 1, hf))
                pos = slice(2 * TILES[hf][0], 2 * TILES[hf][-1] + 2)
                V.tensor_tensor(cT[:, pos, :], cx[:, pos, 0, :], cx[:, pos, 1, :], ALU.mult).then_inc(S("c_done"), 1)
            for hf in range(2):
                dve.wait_ge(S("o_mm"), hf + 1)
                ln_stats(1, o_ps, hf)
            for hf in range(2):
                ln_bias(1, hf)
            dve.wait_ge(S("hbeta_done"), 1)
            for hf in range(2):
                dve.wait_ge(S("on_done"), TILES[hf][-1] + 1)
                sl = TILE_RANGE[hf]
                link(V.tensor_tensor(on[:, sl, :], on[:, sl, :], bc(R_GAMMA).broadcast_to([P, len(TILES[hf]), D]), ALU.mult))
                link(V.tensor_tensor(h2[:, sl, :], on[:, sl, :], hbeta[:, sl, :], ALU.add))
                ln_stats(2, h2_t, hf)
            for hf in range(2):
                ln_bias(2, hf)
                normalise(2, x3_t, h2_t, hf, "x3_dve")
            for hf, (lo, hi) in enumerate(HALVES):
                dve.wait_ge(S("xh_done"), hf + 1)
                V.tensor_tensor(xl[:, lo:hi], ps[2 + hf][:, 0:hi - lo], xh[:, lo:hi], ALU.subtract).then_inc(S("xl_done"), 1)

            def shift_taps():
                dve.wait_ge(S("taps_mm"), 1)
                dve.wait_ge(S("Lf_zero"), 1)
                for k in range(KRC):
                    rows_k = slice(k * QUAD, k * QUAD + E)
                    for hf, (lo, hi) in enumerate(FHALVES):
                        d = (k - KRC // 2) * B
                        a, b = max(lo - d, 0), min(hi - d, N)
                        V.tensor_copy(Lf[rows_k, a:b], ps[6 + hf][rows_k, a + d - lo:b + d - lo]).then_inc(S("taps_done"), 1)

            def router_a():
                dve.wait_ge(S("L_mm"), 1)
                link(V.tensor_tensor(L[:], ps[7][:, 0:NT * E].rearrange("p (i e) -> p i e", e=E),
                                     rows_s[:, R_RC2:R_RC2 + 1, 0:E].broadcast_to([P, NT, E]), ALU.add))
                link(V.tensor_reduce(m1[:], L[:], AX.X, ALU.max))
                V.tensor_tensor(Ld[:], L[:], m1[:].rearrange("p (i o) -> p i o", o=1).broadcast_to([P, NT, E]),
                                ALU.subtract).then_inc(S("Ld_done"), 1)

            def router_b():
                other = L[:].rearrange("p i (o f) -> p i o f", o=1).broadcast_to([P, NT, E, E])
                mine = L[:].rearrange("p i (e o) -> p i e o", o=1).broadcast_to([P, NT, E, E])
                V.tensor_tensor(gt, other, mine, ALU.is_gt)
                link(V.tensor_tensor(eq, other, mine, ALU.is_equal))
                link(V.tensor_tensor(eq, eq, tri_s[:].rearrange("p (o e) f -> p o e f", o=1).broadcast_to([P, NT, E, E]),
                                     ALU.mult))
                link(V.tensor_tensor(gt, gt, eq, ALU.add))
                link(V.tensor_reduce(rank[:], gt, AX.X, ALU.add))
                dve.wait_ge(S("Lx_done"), 1)
                link(V.scalar_tensor_tensor(gates[:], rank[:], 1.5, Lx[:], ALU.is_lt, ALU.mult))
                link(V.tensor_reduce(den[:], gates[:], AX.X, ALU.add))
                link(V.reciprocal(den[:], den[:]))
                V.tensor_tensor(gates[:], gates[:], den[:].rearrange("p (i o) -> p i o", o=1).broadcast_to([P, NT, E]),
                                ALU.mult).then_inc(S("gates_done"), 1)

            def activate(j):
                shared = JOBS[j].expert is None
                dve.wait_ge(S("a2_done"), j + 1)
                if j >= NTT and dve_low(j - NTT):
                    dve.wait_ge(S("hl_dve"), lows(j - NTT, True))
                if j >= NTT and not dve_low(j - NTT):
                    dve.wait_ge(S("hl_pool"), lows(j - NTT, False))
                V.scalar_tensor_tensor(tt[:, j % NTT, :], ex[:, j % 2, :], 1.0, rr[:, j % 2, :],
                                       ALU.add if shared else ALU.min, ALU.mult if shared else ALU.add)\
                    .then_inc(S("tt_done"), 1)

            def high(j):
                dve.wait_ge(S("tt_done"), j + 1)
                if j >= NHID:
                    dve.wait_ge(S("down_mm"), j - NHID + 1)
                V.tensor_copy(hh[:, j % NHID, :, NC1:], halves(tt[:, j % NTT, :])).then_inc(S("hh_done"), 1)

            def low(j):
                part = slice(0, 1 if j == NJ - 1 else 2)
                dve.wait_ge(S("hh_done"), j + 1)
                V.tensor_tensor(hl[:, j % NHID, part, NC1:], halves(tt[:, j % NTT, :])[:, part, :], hh[:, j % NHID, part, NC1:],
                                ALU.subtract).then_inc(S("hl_dve"), 1)

            def unit_end(u):
                dve.wait_ge(S("down_mm"), (u + 1) * HC)
                if u >= 2:
                    dve.wait_ge(S("z_add"), u - 1)
                bank = psum[:, OUT0 + 2 * (u % 2):OUT0 + 2 * (u % 2) + 2, :]
                if u == 0:
                    V.tensor_scalar(halves(yt[0]), bank[:, :, 0:HW], cols_s[:, C_SH2:C_SH2 + 1], None, ALU.add)\
                        .then_inc(S("yt_done"), 1)
                    return
                e = u - 1
                link(V.tensor_tensor(b2c[:, e:e + 1], bank[:, 0, 0:1], cols_s[:, C_E2 + e:C_E2 + e + 1], ALU.add))
                dve.wait_ge(S(f"Gb_in{e % NGB}"), 16 * (e // NGB + 1))
                for part in [slice(0, 2)] if u < NU - 1 else [slice(0, 1), slice(1, 2)]:
                    V.scalar_tensor_tensor(halves(yt[u % 2])[:, part, :], bank[:, part, NC1:NC1 + HW], b2c[:, e:e + 1],
                                           halves(Gb[:, e % NGB, :])[:, part, :], ALU.add, ALU.mult).then_inc(S("yt_done"), 1)

            V.memset(zT, 0.0).then_inc(S("z_zero"), 1)
            V.memset(Lf, 0.0).then_inc(S("Lf_zero"), 1)
            V.memset(hh[:, :, :, 0:NC1].bitcast(F32), -1.0).then_inc(S("z_zero"), 1)
            V.memset(hl[:, :, :, 0:NC1].bitcast(F32), 0.0).then_inc(S("z_zero"), 1)
            for step in range(NJ + END_LAG):
                if step < NJ:
                    activate(step)
                if 1 <= step <= NJ and dve_low(step - 1):
                    low(step - 1)
                if step < NJ:
                    high(step)
                if step == LX_JOB - 1:
                    shift_taps()
                    router_a()
                if step == LX_JOB:
                    router_b()
                if step == 0:
                    link(V.tensor_tensor(h2[:], h2[:], bc(R_LNB).broadcast_to([P, NT, D]), ALU.add))
                if step == GT_STEP:
                    for hf, (lo, hi) in enumerate(HALVES):
                        dve.wait_ge(S("gT_mm"), hf + 1)
                        V.tensor_copy(gatesT[:, lo:hi], ps[6 + hf][0:E, 0:hi - lo]).then_inc(S("gT_done"), 1)
                u = ending(step)
                if u is not None and u != NU - 2:
                    unit_end(u)
                if step == NJ:
                    unit_end(NU - 2)
            for k in range(2):
                dve.wait_ge(S("z_mm"), k + 1)
                ln_stats(3, z_ps, k)
            for k in range(2):
                dve.wait_ge(S("rstd_done"), 6 + k + 1)
                ln_affine(3, z_t, x1_t, z_ps, R_LNG, h2_t, k, "out_done")


def shape_constants():
    c, l = np.divmod(np.arange(R), T)
    head = (l * H + c) // T
    same = (np.arange(H)[:, None] == head[None, :]).astype(np.float32)
    q, k = same, np.where(same > 0, 0.0, NEG).astype(np.float32)
    tri = np.ascontiguousarray(np.broadcast_to(np.tril(np.ones((E, E), np.float32), -1), (P, E, E)))
    taps = np.zeros((KRC, QUAD, E), np.float32)
    taps[:, np.arange(E), np.arange(E)] = 1
    return q, k, np.eye(P, dtype=np.float32), tri, taps.reshape(KRC * QUAD, E)


def kernel(**inputs):
    import numpy as _np
    import concourse.bacc as _bacc
    from concourse import mybir as _mybir
    from concourse.bass_utils import run_bass_kernel_spmd as _run

    a = {k: _np.asarray(v) for k, v in inputs.items()}
    f = lambda n: a["L0_ffn_" + n]
    at = lambda n: a["L0_attn_" + n]
    colv = _np.zeros((P, C_N), _np.float32)
    for n, name in ((C_BQ, "bq"), (C_BK, "bk"), (C_BV, "bv")):
        colv[:, n] = at(name)
    colv[:, C_RC1] = f("rc_b1")
    colv[:, C_SH2] = f("sh_b2")
    colv[:, C_E2:] = f("e_b2").T
    colv[:, C_SH1:C_E1] = f("sh_b1").reshape(HC, P).T
    colv[:, C_E1:C_SH2] = f("e_b1").reshape(E * HC, P).T
    rc2 = _np.zeros(D, _np.float32)
    rc2[:E] = f("rc_b2")
    rowv = _np.stack([a["L0_tok_b"], at("bo"), at("gamma"), at("beta"), rc2, f("ln_g"), f("ln_b")])
    wrc2 = _np.zeros((D, KRC, QUAD), _np.float32)
    wrc2[:, :, :E] = f("rc_w2").transpose(1, 2, 0)
    qmask, kmask, ident, tri, taps = shape_constants()
    laid = {
        "xT": a["x"].reshape(B, LX * FEATS)[:, :JX * P].reshape(B, JX // 2, 2, P).transpose(3, 2, 1, 0),
        "wtok": a["L0_tok_W"].T.reshape(KP, P, D).transpose(1, 0, 2),
        "wqkvo": _np.stack([at("Wq").T, at("Wk").T, at("Wv").T, at("Wo").T], axis=1),
        "wrc1": f("rc_w1").transpose(1, 2, 0),
        "wrc2": wrc2,
        "wsh1": f("sh_w1").transpose(1, 2, 0),
        "wsh2": f("sh_w2")[:, :, 0].T.reshape(HC, P, D).transpose(1, 0, 2),
        "we1": f("e_w1").transpose(1, 0, 2),
        "we2": f("e_w2").reshape(E, HC, P, D).transpose(2, 0, 1, 3),
        "cols": colv,
        "rows": _np.broadcast_to(rowv[None], (P, R_N, D)),
        "qmask": qmask, "kmask": kmask, "ident": ident, "tri": tri, "taps": taps,
    }
    nc = _bacc.Bacc("TRN2", target_bir_lowering=False, num_devices=1)
    arrays, args = {}, []
    for name, v in laid.items():
        v = _np.ascontiguousarray(v)
        arrays[name] = v
        args.append(nc.dram_tensor(name, v.shape, _mybir.dt.from_np(v.dtype), kind="ExternalInput").ap())
    args.append(nc.dram_tensor("out", (B, T, D), F32, kind="ExternalOutput").ap())
    build(nc, *args)
    r = _run(nc, [arrays], core_ids=[0])
    return r.results[0]["out"]
```
